# Optimizing a Trainium2 kernel written in Bass

```python
import numpy as np
import jax
import jax.numpy as jnp

def _softmax(x, axis=-1):
    return jax.nn.softmax(x, axis=axis)

def _gelu(x):
    return jax.nn.gelu(x, approximate=True)

def _silu(x):
    return jax.nn.silu(x)

def _sigmoid(x):
    return jax.nn.sigmoid(x)

def _layernorm(x, axis=-1, eps=1e-05):
    m = jnp.mean(x, axis=axis, keepdims=True)
    v = jnp.var(x, axis=axis, keepdims=True)
    return (x - m) / jnp.sqrt(v + eps)

def _scatter_add(tgt, idx, src, axis=0):
    return tgt.at[idx].add(src)

def _segment_sum(src, seg, n):
    return jax.ops.segment_sum(src, seg, n)
kernel_name = 'mk_decoder_postln_d1_seqx_r8_dc2d18'

def setup_inputs(seed: int=0):
    np.random.seed(seed)
    _w = jnp.asarray

    def _rec_inputs():
        import jax
        import jax.numpy as jnp
        _rk = jax.random.key(seed)
        x = -4.161e-06 + 1 * jax.random.normal(jax.random.fold_in(_rk, 1), (8, 128, 256), jnp.float32)
        _lenS = 128 - jax.random.randint(jax.random.fold_in(_rk, 7), (8,), 0, max(1, 128 // 4) + 1, jnp.int32)
        _lenS2 = 128 - jax.random.randint(jax.random.fold_in(_rk, 8), (8,), 0, max(1, 128 // 4) + 1, jnp.int32)
        _ctx_2048P = jax.random.normal(jax.random.fold_in(_rk, 11), (8, 16, 256), jnp.float32)
        _ctx_2048c = jax.random.dirichlet(jax.random.fold_in(_rk, 511), 0.3 * jnp.ones((16,), jnp.float32), (8, 128))
        _ctx_2048t = jnp.einsum('bsk,bkd->bsd', _ctx_2048c, _ctx_2048P)
        _ctx_2048t = _ctx_2048t * jax.lax.rsqrt(jnp.mean(jnp.square(_ctx_2048t)) + 1e-12) * 0.953939
        ctx_2048 = -0.000192764 + 0.999654 * (_ctx_2048t + 0.3 * jax.random.normal(jax.random.fold_in(_rk, 611), (8, 128, 256), jnp.float32))
        return (x, ctx_2048)
    x, ctx_2048 = _rec_inputs()

    def _L0_attn_setup():
        import jax, jax.numpy as jnp
        import numpy as np
        WIDTH = 256
        NUM_HEADS = 16
        HEAD_DIM = WIDTH // NUM_HEADS
        ROPE_DIMS = HEAD_DIM // 2
        WINDOW = 64
        ROPE_BASE = 10000.0
        NEG_INF = -1000000000.0

        def apply_rope(x, dims, offset=0, base=ROPE_BASE):
            L = x.shape[2]
            half = dims // 2
            pos = (offset + jnp.arange(L)).astype(x.dtype)
            inv_freq = jnp.exp(-jnp.log(jnp.asarray(base, x.dtype)) * (jnp.arange(0, dims, 2).astype(x.dtype) / dims))
            theta = pos[:, None] * inv_freq[None, :]
            cos = jnp.cos(theta)[None, None]
            sin = jnp.sin(theta)[None, None]
            x1 = x[..., :half]
            x2 = x[..., half:dims]
            rest = x[..., dims:]
            rx1 = x1 * cos - x2 * sin
            rx2 = x1 * sin + x2 * cos
            return jnp.concatenate([rx1, rx2, rest], axis=-1)
        key = jax.random.key(seed)
        ks = jax.random.split(key, 6)
        B, L, D, hd = (2, 256, WIDTH, HEAD_DIM)
        x = jax.random.normal(ks[0], (B, L, D), dtype=jnp.float32)
        Wq = jax.random.normal(ks[1], (D, D), dtype=jnp.float32) * 0.02
        Wk = jax.random.normal(ks[2], (D, hd), dtype=jnp.float32) * 0.02
        Wv = jax.random.normal(ks[3], (D, hd), dtype=jnp.float32) * 0.02
        Wo = jax.random.normal(ks[4], (D, D), dtype=jnp.float32) * 0.02
        bo = jax.random.normal(ks[5], (D,), dtype=jnp.float32) * 0.02
        return {'x': x, 'Wq': Wq, 'Wk': Wk, 'Wv': Wv, 'Wo': Wo, 'bo': bo}
    _L0_attn_all = _L0_attn_setup()
    _L0_attn_in = {k: v for k, v in _L0_attn_all.items() if k in ('Wq', 'Wk', 'Wv', 'Wo', 'bo')}
    del _L0_attn_all

    def _L0_xattn_setup():
        import jax, jax.numpy as jnp
        import numpy as np
        FP8_MAX = 448.0
        EPS = 1e-05

        def _fp8_roundtrip(x):
            return x.astype(jnp.float8_e4m3fn).astype(jnp.float32)

        def _div_clamp_fp8(x, scale):
            y = jnp.clip(x.astype(jnp.float32) / scale, -FP8_MAX, FP8_MAX)
            y = y.astype(jnp.bfloat16).astype(jnp.float32)
            return _fp8_roundtrip(y)

        def _ln(x, w, b):
            mu = jnp.mean(x, axis=-1, keepdims=True)
            var = jnp.mean(jnp.square(x - mu), axis=-1, keepdims=True)
            return (x - mu) * jax.lax.rsqrt(var + EPS) * w + b

        def _fp8_linear_pertensor(x, wq, w_scale, in_scale):
            xq = _div_clamp_fp8(x, in_scale)
            return jnp.einsum('bsi,oi->bso', xq * in_scale, wq) * w_scale

        def _gqa(q, k, v):
            scale = 1.0 / np.sqrt(q.shape[-1])
            scores = jnp.einsum('bsghd,btgd->bghst', q, k) * scale
            p = jax.nn.softmax(scores, axis=-1)
            return jnp.einsum('bghst,btgd->bsghd', p, v)
        key = jax.random.key(seed)
        ks = jax.random.split(key, 8)
        B, S, SC, H, NH, G, D = (2, 256, 64, 256, 16, 8, 128)

        def qw(k, out_f, in_f):
            w = jax.random.normal(k, (out_f, in_f), jnp.float32) * 0.02
            sc = jnp.max(jnp.abs(w)) / FP8_MAX
            return (_fp8_roundtrip(w / sc), sc.astype(jnp.float32))
        wq, wq_s = qw(ks[0], NH * D, H)
        wqx, wqx_s = qw(ks[1], NH * D, H)
        wk, wk_s = qw(ks[2], G * D, H)
        wv, wv_s = qw(ks[3], G * D, H)
        wproj, wp_s = qw(ks[4], H, 2 * NH * D)
        return {'hidden_states': jax.random.normal(ks[5], (B, S, H), jnp.float32), 'cond': jax.random.normal(ks[6], (B, SC, H), jnp.float32), 'ln_w': jnp.ones((H,), jnp.float32), 'ln_b': jnp.zeros((H,), jnp.float32), 'wq': wq, 'wq_scale': wq_s, 'q_in_scale': jnp.full((H,), 0.05, jnp.float32), 'wqx': wqx, 'wqx_scale': wqx_s, 'qx_in_scale': jnp.full((H,), 0.05, jnp.float32), 'wk': wk, 'wk_scale': wk_s, 'k_in_scale': jnp.full((H,), 0.05, jnp.float32), 'wv': wv, 'wv_scale': wv_s, 'v_in_scale': jnp.full((H,), 0.05, jnp.float32), 'w_kv_x': jax.random.normal(ks[7], (2 * G * D, H), jnp.float32) * 0.02, 'qln_w': jnp.ones((D,), jnp.float32), 'qln_b': jnp.zeros((D,), jnp.float32), 'kln_w': jnp.ones((D,), jnp.float32), 'kln_b': jnp.zeros((D,), jnp.float32), 'qxln_w': jnp.ones((D,), jnp.float32), 'qxln_b': jnp.zeros((D,), jnp.float32), 'kxln_w': jnp.ones((D,), jnp.float32), 'kxln_b': jnp.zeros((D,), jnp.float32), 'wproj': wproj, 'proj_w_scale': wp_s, 'proj_in_scale': jnp.asarray(0.05, jnp.float32), 'proj_smooth': jnp.full((2 * NH * D,), 0.05, jnp.float32)}
    _L0_xattn_all = _L0_xattn_setup()
    _L0_xattn_in = {k: v for k, v in _L0_xattn_all.items() if k in ('ln_w', 'ln_b', 'wq', 'wq_scale', 'q_in_scale', 'wqx', 'wqx_scale', 'qx_in_scale', 'wk', 'wk_scale', 'k_in_scale', 'wv', 'wv_scale', 'v_in_scale', 'w_kv_x', 'qln_w', 'qln_b', 'kln_w', 'kln_b', 'qxln_w', 'qxln_b', 'kxln_w', 'kxln_b', 'wproj', 'proj_w_scale', 'proj_in_scale', 'proj_smooth')}
    del _L0_xattn_all

    def _L0_ffn_setup():
        import jax, jax.numpy as jnp
        import numpy as np
        B, S, H, I, E, K = (4, 256, 256, 512, 8, 2)
        key = jax.random.key(seed)
        k1, k2, k3, k4 = jax.random.split(key, 4)
        return {'hidden_states': jax.random.normal(k1, (B, S, H), dtype=jnp.float32), 'gate_weight': jax.random.normal(k2, (E, H), dtype=jnp.float32) * 0.02, 'gate_up_proj': jax.random.normal(k3, (E, 2 * I, H), dtype=jnp.float32) * 0.02, 'down_proj': jax.random.normal(k4, (E, H, I), dtype=jnp.float32) * 0.02}
    _L0_ffn_all = _L0_ffn_setup()
    _L0_ffn_in = {k: v for k, v in _L0_ffn_all.items() if k in ('gate_weight', 'gate_up_proj', 'down_proj')}
    del _L0_ffn_all
    return {'x': x, 'ctx_2048': ctx_2048, 'L0_attn_Wq': _L0_attn_in['Wq'], 'L0_attn_Wk': _L0_attn_in['Wk'], 'L0_attn_Wv': _L0_attn_in['Wv'], 'L0_attn_Wo': _L0_attn_in['Wo'], 'L0_attn_bo': _L0_attn_in['bo'], 'L0_xattn_ln_w': _L0_xattn_in['ln_w'], 'L0_xattn_ln_b': _L0_xattn_in['ln_b'], 'L0_xattn_wq': _L0_xattn_in['wq'], 'L0_xattn_wq_scale': _L0_xattn_in['wq_scale'], 'L0_xattn_q_in_scale': _L0_xattn_in['q_in_scale'], 'L0_xattn_wqx': _L0_xattn_in['wqx'], 'L0_xattn_wqx_scale': _L0_xattn_in['wqx_scale'], 'L0_xattn_qx_in_scale': _L0_xattn_in['qx_in_scale'], 'L0_xattn_wk': _L0_xattn_in['wk'], 'L0_xattn_wk_scale': _L0_xattn_in['wk_scale'], 'L0_xattn_k_in_scale': _L0_xattn_in['k_in_scale'], 'L0_xattn_wv': _L0_xattn_in['wv'], 'L0_xattn_wv_scale': _L0_xattn_in['wv_scale'], 'L0_xattn_v_in_scale': _L0_xattn_in['v_in_scale'], 'L0_xattn_w_kv_x': _L0_xattn_in['w_kv_x'], 'L0_xattn_qln_w': _L0_xattn_in['qln_w'], 'L0_xattn_qln_b': _L0_xattn_in['qln_b'], 'L0_xattn_kln_w': _L0_xattn_in['kln_w'], 'L0_xattn_kln_b': _L0_xattn_in['kln_b'], 'L0_xattn_qxln_w': _L0_xattn_in['qxln_w'], 'L0_xattn_qxln_b': _L0_xattn_in['qxln_b'], 'L0_xattn_kxln_w': _L0_xattn_in['kxln_w'], 'L0_xattn_kxln_b': _L0_xattn_in['kxln_b'], 'L0_xattn_wproj': _L0_xattn_in['wproj'], 'L0_xattn_proj_w_scale': _L0_xattn_in['proj_w_scale'], 'L0_xattn_proj_in_scale': _L0_xattn_in['proj_in_scale'], 'L0_xattn_proj_smooth': _L0_xattn_in['proj_smooth'], 'L0_ffn_gate_weight': _L0_ffn_in['gate_weight'], 'L0_ffn_gate_up_proj': _L0_ffn_in['gate_up_proj'], 'L0_ffn_down_proj': _L0_ffn_in['down_proj']}

def reference(x, ctx_2048, L0_attn_Wq, L0_attn_Wk, L0_attn_Wv, L0_attn_Wo, L0_attn_bo, L0_xattn_ln_w, L0_xattn_ln_b, L0_xattn_wq, L0_xattn_wq_scale, L0_xattn_q_in_scale, L0_xattn_wqx, L0_xattn_wqx_scale, L0_xattn_qx_in_scale, L0_xattn_wk, L0_xattn_wk_scale, L0_xattn_k_in_scale, L0_xattn_wv, L0_xattn_wv_scale, L0_xattn_v_in_scale, L0_xattn_w_kv_x, L0_xattn_qln_w, L0_xattn_qln_b, L0_xattn_kln_w, L0_xattn_kln_b, L0_xattn_qxln_w, L0_xattn_qxln_b, L0_xattn_kxln_w, L0_xattn_kxln_b, L0_xattn_wproj, L0_xattn_proj_w_scale, L0_xattn_proj_in_scale, L0_xattn_proj_smooth, L0_ffn_gate_weight, L0_ffn_gate_up_proj, L0_ffn_down_proj):
    import jax
    import jax.numpy as jnp

    def _L0_attn_ref(x, Wq, Wk, Wv, Wo, bo):
        import jax, jax.numpy as jnp
        import numpy as np
        WIDTH = 256
        NUM_HEADS = 16
        HEAD_DIM = WIDTH // NUM_HEADS
        ROPE_DIMS = HEAD_DIM // 2
        WINDOW = 64
        ROPE_BASE = 10000.0
        NEG_INF = -1000000000.0

        def apply_rope(x, dims, offset=0, base=ROPE_BASE):
            L = x.shape[2]
            half = dims // 2
            pos = (offset + jnp.arange(L)).astype(x.dtype)
            inv_freq = jnp.exp(-jnp.log(jnp.asarray(base, x.dtype)) * (jnp.arange(0, dims, 2).astype(x.dtype) / dims))
            theta = pos[:, None] * inv_freq[None, :]
            cos = jnp.cos(theta)[None, None]
            sin = jnp.sin(theta)[None, None]
            x1 = x[..., :half]
            x2 = x[..., half:dims]
            rest = x[..., dims:]
            rx1 = x1 * cos - x2 * sin
            rx2 = x1 * sin + x2 * cos
            return jnp.concatenate([rx1, rx2, rest], axis=-1)
        B, L, D = x.shape
        H, hd = (NUM_HEADS, HEAD_DIM)
        scale = hd ** (-0.5)
        q = (x @ Wq).reshape(B, L, H, hd).transpose(0, 2, 1, 3)
        k = (x @ Wk).reshape(B, L, 1, hd).transpose(0, 2, 1, 3)
        v = (x @ Wv).reshape(B, L, 1, hd).transpose(0, 2, 1, 3)
        q = apply_rope(q, ROPE_DIMS)
        k = apply_rope(k, ROPE_DIMS)
        i = jnp.arange(L)[:, None]
        j = jnp.arange(L)[None, :]
        allowed = (i - j >= 0) & (i - j < WINDOW)
        mask = jnp.where(allowed, 0.0, NEG_INF).astype(x.dtype)
        scores = jnp.einsum('bhqd,bkd->bhqk', q, k[:, 0]) * scale
        scores = scores + mask[None, None]
        attn = jax.nn.softmax(scores, axis=-1)
        out = jnp.einsum('bhqk,bkd->bhqd', attn, v[:, 0])
        out = out.transpose(0, 2, 1, 3).reshape(B, L, D)
        return out @ Wo + bo

    def _L0_xattn_ref(hidden_states, cond, ln_w, ln_b, wq, wq_scale, q_in_scale, wqx, wqx_scale, qx_in_scale, wk, wk_scale, k_in_scale, wv, wv_scale, v_in_scale, w_kv_x, qln_w, qln_b, kln_w, kln_b, qxln_w, qxln_b, kxln_w, kxln_b, wproj, proj_w_scale, proj_in_scale, proj_smooth):
        import jax, jax.numpy as jnp
        import numpy as np
        FP8_MAX = 448.0
        EPS = 1e-05

        def _fp8_roundtrip(x):
            return x.astype(jnp.float8_e4m3fn).astype(jnp.float32)

        def _div_clamp_fp8(x, scale):
            y = jnp.clip(x.astype(jnp.float32) / scale, -FP8_MAX, FP8_MAX)
            y = y.astype(jnp.bfloat16).astype(jnp.float32)
            return _fp8_roundtrip(y)

        def _ln(x, w, b):
            mu = jnp.mean(x, axis=-1, keepdims=True)
            var = jnp.mean(jnp.square(x - mu), axis=-1, keepdims=True)
            return (x - mu) * jax.lax.rsqrt(var + EPS) * w + b

        def _fp8_linear_pertensor(x, wq, w_scale, in_scale):
            xq = _div_clamp_fp8(x, in_scale)
            return jnp.einsum('bsi,oi->bso', xq * in_scale, wq) * w_scale

        def _gqa(q, k, v):
            scale = 1.0 / np.sqrt(q.shape[-1])
            scores = jnp.einsum('bsghd,btgd->bghst', q, k) * scale
            p = jax.nn.softmax(scores, axis=-1)
            return jnp.einsum('bghst,btgd->bsghd', p, v)
        b, s, _ = hidden_states.shape
        sc = cond.shape[1]
        d = qln_w.shape[0]
        nh = wq.shape[0] // d
        g = wk.shape[0] // d
        hpg = nh // g
        ln_out = _ln(hidden_states, ln_w, ln_b)
        q = _fp8_linear_pertensor(ln_out, wq, wq_scale, q_in_scale).reshape(b, s, g, hpg, d)
        q = _ln(q, qln_w, qln_b)
        k = _fp8_linear_pertensor(ln_out, wk, wk_scale, k_in_scale).reshape(b, s, g, d)
        k = _ln(k, kln_w, kln_b)
        v = _fp8_linear_pertensor(ln_out, wv, wv_scale, v_in_scale).reshape(b, s, g, d)
        core = _gqa(q, k, v).reshape(b, s, nh * d)
        qx = _fp8_linear_pertensor(ln_out, wqx, wqx_scale, qx_in_scale).reshape(b, s, g, hpg, d)
        qx = _ln(qx, qxln_w, qxln_b)
        kvx = jnp.einsum('bsi,oi->bso', cond, w_kv_x)
        kx, vx = jnp.split(kvx, 2, axis=-1)
        kx = _ln(kx.reshape(b, sc, g, d), kxln_w, kxln_b)
        vx = vx.reshape(b, sc, g, d)
        xout = _gqa(qx, kx, vx).reshape(b, s, nh * d)
        cat = jnp.concatenate([core, xout], axis=-1)
        catq = _div_clamp_fp8(cat, proj_smooth)
        return jnp.einsum('bsi,oi->bso', catq, wproj) * (proj_in_scale * proj_w_scale)

    def _L0_ffn_ref(hidden_states, gate_weight, gate_up_proj, down_proj):
        import jax, jax.numpy as jnp
        import numpy as np
        B, S, H, I, E, K = (4, 256, 256, 512, 8, 2)
        b, s, h = hidden_states.shape
        num_experts, top_k = (gate_weight.shape[0], K)
        x = hidden_states.reshape(-1, h)
        router_logits = x @ gate_weight.T
        probs = jax.nn.softmax(router_logits.astype(jnp.float32), axis=-1)
        top_v, top_i = jax.lax.top_k(probs, top_k)
        top_v = top_v / top_v.sum(axis=-1, keepdims=True)
        combine_w = jnp.einsum('tke,tk->te', jax.nn.one_hot(top_i, num_experts, dtype=top_v.dtype), top_v).astype(x.dtype)

        def expert_step(acc, inp):
            gu, dp, w = inp
            gate, up = jnp.split(x @ gu.T, 2, axis=-1)
            hidden = jax.nn.silu(gate) * up
            y = hidden @ dp.T
            return (acc + w[:, None] * y, None)
        out, _ = jax.lax.scan(expert_step, jnp.zeros_like(x), (gate_up_proj, down_proj, combine_w.T))
        return out.reshape(b, s, h)
    x = _layernorm(x + _L0_attn_ref(x, L0_attn_Wq, L0_attn_Wk, L0_attn_Wv, L0_attn_Wo, L0_attn_bo), axis=-1)
    x = _layernorm(x + _L0_xattn_ref(x, ctx_2048, L0_xattn_ln_w, L0_xattn_ln_b, L0_xattn_wq, L0_xattn_wq_scale, L0_xattn_q_in_scale, L0_xattn_wqx, L0_xattn_wqx_scale, L0_xattn_qx_in_scale, L0_xattn_wk, L0_xattn_wk_scale, L0_xattn_k_in_scale, L0_xattn_wv, L0_xattn_wv_scale, L0_xattn_v_in_scale, L0_xattn_w_kv_x, L0_xattn_qln_w, L0_xattn_qln_b, L0_xattn_kln_w, L0_xattn_kln_b, L0_xattn_qxln_w, L0_xattn_qxln_b, L0_xattn_kxln_w, L0_xattn_kxln_b, L0_xattn_wproj, L0_xattn_proj_w_scale, L0_xattn_proj_in_scale, L0_xattn_proj_smooth), axis=-1)
    x = _layernorm(x + _L0_ffn_ref(x, L0_ffn_gate_weight, L0_ffn_gate_up_proj, L0_ffn_down_proj), axis=-1)
    return x

_drawn_inputs = setup_inputs


def setup_inputs(seed=0):
    import zlib

    import numpy as np

    out = dict(_drawn_inputs(seed))
    spreads = {'L0_xattn_ln_w': (1.0, 0.6),
     'L0_xattn_ln_b': (0.0, 0.1),
     'L0_xattn_q_in_scale': (0.05000000074505806, 0.6),
     'L0_xattn_qx_in_scale': (0.05000000074505806, 0.6),
     'L0_xattn_k_in_scale': (0.05000000074505806, 0.6),
     'L0_xattn_v_in_scale': (0.05000000074505806, 0.6),
     'L0_xattn_qln_w': (1.0, 0.6),
     'L0_xattn_qln_b': (0.0, 0.8),
     'L0_xattn_kln_w': (1.0, 0.6),
     'L0_xattn_kln_b': (0.0, 0.8),
     'L0_xattn_qxln_w': (1.0, 0.6),
     'L0_xattn_qxln_b': (0.0, 0.8),
     'L0_xattn_kxln_w': (1.0, 0.6),
     'L0_xattn_kxln_b': (0.0, 0.8),
     'L0_xattn_proj_smooth': (0.05000000074505806, 0.2)}
    factors = {'L0_attn_Wq': 8.0,
     'L0_attn_Wk': 8.0,
     'L0_ffn_gate_weight': 3.83,
     'L0_ffn_gate_up_proj': 3.307,
     'L0_ffn_down_proj': 3.318}
    for name, (base, spread) in spreads.items():
        noise = np.random.default_rng([zlib.crc32(name.encode()), seed]).standard_normal(out[name].shape)
        drawn = base * np.exp(spread * noise) if base else spread * noise
        out[name] = jnp.asarray(drawn.astype(out[name].dtype))
    for name, factor in factors.items():
        out[name] = (out[name] * factor).astype(out[name].dtype)
    return out
```

```python
from contextlib import ExitStack

import numpy as np

import concourse.bass as bass
from concourse import mybir

F32 = mybir.dt.float32
F32R = mybir.dt.float32r
BF16 = mybir.dt.bfloat16
U16 = mybir.dt.uint16
NO_SIGN = 0x7FFF
ALU = mybir.AluOpType
ACT = mybir.ActivationFunctionType
AX = mybir.AxisListType.X

P = 128
B, L, D = 8, 128, 256
C = D // P
H1, HD1 = 16, 16
ROT = HD1 // 4
WINDOW = 64
G, DH = 8, 128
E, I = 8, 512
IC = I // P
NVAR = 4
EPS = 1e-5
FP8_MAX = 448.0
FP8_MIN_EXP = 1.5 * 2.0 ** -6
FP8_SHIFT = 2.0 ** 20
QKV1 = D + 2 * HD1
WCOLS = 1024
WPIECES = 3
WALL = WPIECES * WCOLS + 4

_at = 0
COL = {}
for _name, _n in (("ident", P), ("mask", P), ("cos", ROT), ("sin", ROT), ("head", 8), ("ln_w", C), ("ln_b", C),
                  ("in_scale", C * NVAR), ("qk_ln", 8), ("w_scale", NVAR), ("proj", 2), ("bo", D),
                  ("wqkv", C * QKV1), ("wo", C * D), ("gate", C * E), ("rank", E)):
    COL[_name] = (_at, _at + _n)
    _at += _n
SMALL = _at


def need(eng, sem, value):
    if isinstance(value, int) and value <= 0:
        return
    eng.wait_ge(sem, value)


class Chain:

    def __init__(self, eng, sem, per_item, item):
        self.eng, self.sem, self.per, self.base, self.k = eng, sem, per_item, item * per_item, 0

    def __call__(self, ins, settle=None):
        self.k += 1
        assert self.k <= self.per
        ins.then_inc(self.sem, 1)
        self.eng.wait_ge(self.sem, self.base + self.k)
        if settle:
            settle()


def live(item, count):
    return not isinstance(item, int) or 0 <= item < count


def decoder_layer(nc, x, xT, ctxT, small, wall, out):
    ctx = ExitStack()
    with ctx:
        def sb(name, cols, dt=F32):
            return ctx.enter_context(nc.sbuf_tensor(name, [P] + list(cols), dt))

        def sem(name):
            return ctx.enter_context(nc.semaphore(name))

        bank = [ctx.enter_context(nc.psum_tensor(f"bank{i}", [P, 512], F32)) for i in range(8)]

        sm = sb("small_sb", [SMALL])
        col = {k: sm[:, a:b] for k, (a, b) in COL.items()}
        x_all = sb("x_all", [B * D])
        x1_all = sb("x1_all", [B * D])
        y_all = sb("y_all", [B, D])
        xq = sb("xq", [C * NVAR, B * L], F32R)
        ctx_hl = sb("ctx_hl", [2, C, B * L], F32R)
        raw = sb("raw", [WALL])
        w_hi = sb("w_hi", [2, WPIECES * WCOLS], F32R)
        w_lo = sb("w_lo", [2, WPIECES * WCOLS], F32R)
        neg_half = sb("neg_half", [8])
        mask_b = sb("mask_b", [512], BF16)
        ident_b = sb("ident_b", [P], BF16)
        inv_in = sb("inv_in", [C * NVAR])
        w_mul = sb("w_mul", [G + 1, C * NVAR])
        inv_smooth = sb("inv_smooth", [2, 4])
        proj_c = sb("proj_c", [1])
        seen = sb("seen", [1])
        one16 = sb("one16", [HD1])
        xT_in = sb("xT_in", [C, L])
        qkv_raw = sb("qkv_raw", [QKV1])
        rope_t = sb("rope_t", [4, 17, ROT])
        k_rep = sb("k_rep", [8, HD1])
        v_one = sb("v_one", [HD1 + 1])
        qT1 = sb("qT1", [C, L])
        k_bd = sb("k_bd", [8, L])
        p_sb = sb("p_sb", [4, 512])
        pT1 = sb("pT1", [4, 512])
        mx1 = sb("mx1", [4, 4])
        rden1 = sb("rden1", [H1])
        o_sb = sb("o_sb", [D])
        oT_sb = sb("oT_sb", [C, L])
        xb = sb("xb", [D])
        ax = sb("ax", [D])
        z2 = sb("z2", [D])
        lnT = sb("lnT", [C, L])
        bn = sb("bn", [6])
        mv = sb("mv", [2])
        ve = sb("ve", [1])
        rstd = sb("rstd", [1])
        q_y = sb("q_y", [C * NVAR * L], BF16)
        q_m = sb("q_m", [C * NVAR * L], BF16)
        q_p = sb("q_p", [C * NVAR * L])
        st = sb("st", [6, 6])
        sum_m2 = sb("sum_m2", [6, 2])
        ag = sb("ag", [4, 6])
        mean6 = sb("mean6", [6])
        rstd6 = sb("rstd6", [6])
        nb6 = sb("nb6", [6])
        z_self = sb("z_self", [3, DH])
        z_cross = sb("z_cross", [3, DH])
        t_self = sb("t_self", [3, L])
        t_cross = sb("t_cross", [3, L])
        v_ring = sb("v_ring", [4, 2, DH])
        mx2 = sb("mx2", [4, 4])
        sums = sb("sums", [4, 4])
        rden2 = sb("rden2", [4, 4])
        pT2 = sb("pT2", [512])
        c_raw = sb("c_raw", [512], BF16)
        c_y = sb("c_y", [512], BF16)
        c_m = sb("c_m", [512], BF16)
        c_p = sb("c_p", [512])
        cat_q = sb("cat_q", [2, 4, L], F32R)
        x2_t = sb("x2_t", [D])
        x2T_t = sb("x2T_t", [C, L])
        logits = sb("logits", [B * E])
        comb = sb("comb", [B, E])
        rt = sb("rt", [8, B * E])
        r1 = sb("r1", [6, B])
        s_sb, h_sb = pT1[:, 0:2, :], pT1[:, 2:4, :]

        S = {n: sem(n) for n in (
            "small_in x_in ctx_in xT_in_s w_in out_done "
            "consts neg_ready mul_ready v_ones inv_ready mask_ready pool_c "
            "w_scaled w_hi_done w_lo_done ctx_hi ctx_lo "
            "qkv_done qkv_copied roped rope_c turned1 qT_ready kbd_ready scores1 max1 shifted1 exp1 "
            "pT_done1 pT_copied1 v_ready pv_done1 rden_c o_ready oT_done oT_copied attn_done xb_ready "
            "ax_ready ln_c var_ready rstd_ready z2_ready zT_done zT_copied q_c abs_c quant_ready qp_c xq_done "
            "proj_a proj_b agg_c var2 rstd2 nb_ready norm_a norm_b turn_a turn_b ev_a ev_b scores2 max2 shifted2 "
            "exp2 sum_c rden_ready probs_ready pT_done2 pT_copied2 pv_done2 cat_raw cq_c cat_m cp_c cat_ready "
            "out_proj y_added pool_copy "
            "x2_c x2_var x2_rstd x2_ready x2_turned x2T_ready x2_hi x2_lo x2_kept router logits_in route_c "
            "comb_ready gate_up silu_done h_ready h_hi h_lo down_done acc_added "
            "f_c f_var f_rstd out_ready").split()}

        block = ctx.enter_context(nc.Block())

        def settle():
            nc.vector.tensor_copy(seen[:, :], proj_c[:, :])

        def ds(start, n):
            return bass.ds(start, n)

        LAG1 = 3

        def attention_slots(eng, slot):
            for n in range(LAG1):
                slot(n)
            with eng.Fori(LAG1, B) as n:
                slot(n)
            for n in range(B, B + LAG1):
                slot(n)

        ITEMS = G * B
        SPAN = 2 * B
        LAG2 = 7

        def group_slots(eng, slot):
            for j in range(SPAN):
                slot(j, j, 0)
            with eng.Fori(1, G // 2) as r:
                for j in range(SPAN):
                    slot(r * SPAN + j, j, r * 2)
            for j in range(LAG2):
                slot(ITEMS + j, j, G)

        ESPAN = 4

        def expert_slots(eng, slot):
            for j in range(ESPAN):
                slot(j, j, 0)
            with eng.Fori(1, E // 2) as r:
                for j in range(ESPAN):
                    slot(r * ESPAN + j, j, r * 2)
            slot(2 * E, 0, E)

        def expert_slots_split(eng, slot):
            for j in range(ESPAN):
                slot(j, j, 0)
            with eng.Fori(1, E // 2 - 1) as r:
                for j in range(ESPAN):
                    slot(r * ESPAN + j, j, r * 2)
            for j in range(ESPAN + 1):
                slot(2 * E - ESPAN + j, j, E - 2)

        def hidden_parts():
            a = [xq[:, (2 + k) * C:(3 + k) * C, :].rearrange("p c t -> p (c t)").rearrange("p (i t) -> p i t", i=IC) for k in range(2)]
            b = [ctx_hl[:, k, :, :].rearrange("p c t -> p (c t)").rearrange("p (i t) -> p i t", i=IC) for k in range(2)]
            return a, b

        @block.sync
        def _(sp):
            sp.dma_start(sm[:, :], small).then_inc(S["small_in"], 16)
            sp.dma_start(xT_in[:, :, :], xT[0]).then_inc(S["xT_in_s"], 16)
            sp.dma_start(x_all[:, :].rearrange("p (b d) -> p b d", b=B), x.rearrange("b p d -> p b d")).then_inc(S["x_in"], 16)
            sp.dma_start(raw[:, :], wall[0]).then_inc(S["w_in"], 16)
            sp.dma_start(x1_all[:, 0:B * L], ctxT[0]).then_inc(S["ctx_in"], 16)
            sp.dma_start(y_all[:, :, :].rearrange("p b d -> p (b d)")[:, 0:B * L], ctxT[1]).then_inc(S["ctx_in"], 16)

            with sp.Fori(1, B) as n:
                sp.wait_ge(S["qkv_done"], n)
                sp.dma_start(xT_in[:, :, :], xT[ds(n, 1)].rearrange("o p c l -> p (o c) l")).then_inc(S["xT_in_s"], 16)
            with sp.Fori(1, G + E) as g:
                sp.wait_ge(S["w_lo_done"], g * WPIECES)
                sp.wait_ge(S["w_hi_done"], g * WPIECES)
                sp.dma_start(raw[:, :], wall[ds(g, 1)].rearrange("o p c -> p (o c)")).then_inc(S["w_in"], 16)
            with sp.Fori(0, B) as b:
                sp.wait_ge(S["out_ready"], b + 1)
                sp.dma_start(out[ds(b, 1)].rearrange("o p d -> p (o d)"), x_all[:, ds(b * D, D)]).then_inc(S["out_done"], 16)
            sp.wait_ge(S["out_done"], 16 * B)

        @block.tensor
        def _(pe):
            ident = col["ident"]
            wqkv = col["wqkv"].rearrange("p (c n) -> p c n", c=C)
            wo = col["wo"].rearrange("p (c n) -> p c n", c=C)
            gate = col["gate"].rearrange("p (c e) -> p c e", c=C)

            def scores_bank(m, j):
                if j == 0:
                    need(pe, S["qT_ready"], m + 1)
                    need(pe, S["kbd_ready"], m + 1)
                need(pe, S["shifted1"], 4 * m + j - 1)
                to = bank[2 + j % 2][:, :]
                nc.tensor.matmul(to, qT1[:, j // 2, :], k_bd[:, 4 * (j % 2):4 * (j % 2) + 4, :], start=True, stop=False)
                nc.tensor.matmul(to, ident_b[:, :], mask_b[:, :], start=False, stop=True).then_inc(S["scores1"], 1)

            def turn_probs(m, j):
                need(pe, S["exp1"], 4 * m + j + 1)
                need(pe, S["pT_copied1"], 4 * m + j - 1)
                for i in range(4):
                    t = nc.tensor.transpose(bank[4 + j % 2][:, i * P:(i + 1) * P], p_sb[:, j, i * P:(i + 1) * P], ident)
                t.then_inc(S["pT_done1"], 1)

            def values1(m, j):
                if j == 0:
                    need(pe, S["o_ready"], m)
                    need(pe, S["v_ready"], m + 1)
                need(pe, S["pT_copied1"], 4 * m + j + 1)
                for i in range(4):
                    h = 4 * j + i
                    t = nc.tensor.matmul(bank[6][:, h * 17:(h + 1) * 17], pT1[:, j, i * P:(i + 1) * P], v_one[:, :],
                                         start=True, stop=True)
                if j == 3:
                    t.then_inc(S["pv_done1"], 1)

            def slot1(n):
                a, b, z = n - 1, n - 2, n - 3
                if live(z, B):
                    need(pe, S["z2_ready"], z + 1)
                    for c in range(C):
                        t = nc.tensor.transpose(bank[7][:, c * P:(c + 1) * P], z2[:, c * P:(c + 1) * P], ident)
                    t.then_inc(S["zT_done"], 1)
                if live(n, B):
                    if isinstance(n, int) and n == 0:
                        pe.wait_ge(S["small_in"], 16)
                        pe.wait_ge(S["mask_ready"], 2)
                    need(pe, S["xT_in_s"], 16 * (n + 1))
                    need(pe, S["qkv_copied"], n)
                    for c in range(C):
                        t = nc.tensor.matmul(bank[0][:, 0:QKV1], xT_in[:, c, :], wqkv[:, c, :], start=(c == 0), stop=(c == C - 1))
                    t.then_inc(S["qkv_done"], 1)
                if live(a, B):
                    scores_bank(a, 0)
                    scores_bank(a, 1)
                if live(b, B):
                    need(pe, S["o_ready"], b + 1)
                    need(pe, S["zT_copied"], b)
                    for c in range(C):
                        t = nc.tensor.transpose(bank[7][:, c * P:(c + 1) * P], o_sb[:, c * P:(c + 1) * P], ident)
                    t.then_inc(S["oT_done"], 1)
                if live(a, B):
                    scores_bank(a, 2)
                    turn_probs(a, 0)
                if live(n, B):
                    need(pe, S["roped"], n + 1)
                    need(pe, S["kbd_ready"], n)
                    for c in range(C):
                        nc.tensor.transpose(bank[1][:, c * P:(c + 1) * P], qkv_raw[:, c * P:(c + 1) * P], ident)
                    nc.tensor.transpose(bank[1][:, D:D + P], k_rep[:, :, :].rearrange("p a b -> p (a b)"), ident).then_inc(S["turned1"], 1)
                if live(a, B):
                    scores_bank(a, 3)
                    turn_probs(a, 1)
                if live(b, B):
                    need(pe, S["oT_copied"], b + 1)
                    for c in range(C):
                        t = nc.tensor.matmul(bank[7][:, 0:D], oT_sb[:, c, :], wo[:, c, :], start=(c == 0), stop=(c == C - 1))
                    t.then_inc(S["attn_done"], 1)
                if live(a, B):
                    turn_probs(a, 2)
                    values1(a, 0)
                    values1(a, 1)
                    turn_probs(a, 3)
                    values1(a, 2)
                    values1(a, 3)

            attention_slots(pe, slot1)

            def slot2(n, j, g0):
                def has(k):
                    return live(n - k, ITEMS)

                par = (j // B) % 2
                bt = (j % B) * L
                hi, lo = w_hi[:, par, :], w_lo[:, par, :]
                bank_a, bank_b = bank[2 * (j % 2)], bank[2 * (j % 2) + 1]

                def turn_qk(m, z, src, inc, free, count):
                    need(pe, S[src], m + 1)
                    need(pe, S[free], count)
                    for i in range(3):
                        t = nc.tensor.transpose(bank[4][:, i * P:(i + 1) * P], z[:, i, :], ident)
                    t.then_inc(S[inc], 1)

                if has(2):
                    turn_qk(n - 2, z_self, "norm_a", "turn_a", "ev_b", n - 2)
                if has(0):
                    if j % B == 0:
                        g = g0 + j // B
                        pe.wait_ge(S["w_hi_done"], WPIECES * (g + 1))
                        pe.wait_ge(S["w_lo_done"], WPIECES * (g + 1))
                        if isinstance(n, int) and n == 0:
                            pe.wait_ge(S["xq_done"], B)
                            pe.wait_ge(S["ctx_hi"], C)
                            pe.wait_ge(S["ctx_lo"], C)
                            pe.wait_ge(S["zT_copied"], B)
                            pe.wait_ge(S["ax_ready"], B)
                    need(pe, S["norm_a"], n - 1)
                    for var, at, w in ((0, 0, 256), (1, 256, 128), (2, 384, 128)):
                        for c in range(C):
                            for k, part in enumerate((hi, lo)):
                                t = nc.tensor.matmul(bank_a[:, at:at + w], xq[:, c * NVAR + var, bt:bt + L],
                                                     part[:, c * WCOLS + at:c * WCOLS + at + w],
                                                     start=(c == 0 and k == 0), stop=(c == C - 1 and k == 1))
                    t.then_inc(S["proj_a"], 1)
                if has(4):
                    m = n - 4
                    need(pe, S["probs_ready"], m + 1)
                    need(pe, S["y_added"], m - 2)
                    for i in range(4):
                        t = nc.tensor.transpose(bank[6][:, i * P:(i + 1) * P], p_sb[:, (j - 4) % 4, i * P:(i + 1) * P], ident)
                    t.then_inc(S["pT_done2"], 1)
                if has(2):
                    turn_qk(n - 2, z_cross, "norm_b", "turn_b", "ev_a", n - 1)
                if has(0):
                    need(pe, S["norm_b"], n - 1)
                    for c in range(C):
                        for k, part in enumerate((hi, lo)):
                            nc.tensor.matmul(bank_b[:, 0:256], xq[:, c * NVAR + 3, bt:bt + L],
                                             part[:, c * WCOLS + 512:c * WCOLS + 768],
                                             start=(c == 0 and k == 0), stop=(c == C - 1 and k == 1))
                    parts = [(c, a, w) for c in range(C) for a, w in ((0, hi), (0, lo), (1, hi))]
                    for i, (c, a, w) in enumerate(parts):
                        t = nc.tensor.matmul(bank_b[:, 256:512], ctx_hl[:, a, c, bt:bt + L],
                                             w[:, c * WCOLS + 768:c * WCOLS + 1024], start=(i == 0), stop=(i == len(parts) - 1))
                    t.then_inc(S["proj_b"], 1)
                if has(4):
                    m = n - 4
                    need(pe, S["pT_copied2"], m + 1)
                    need(pe, S["cat_raw"], m)
                    for i in range(2):
                        t = nc.tensor.matmul(bank[7][:, i * 256:(i + 1) * 256], v_ring[:, (j - 4) % 4, i, :],
                                             pT2[:, i * 256:(i + 1) * 256], start=True, stop=True)
                    t.then_inc(S["pv_done2"], 1)
                if has(6):
                    m = n - 6
                    part = ((j - 6) // B) % 2
                    need(pe, S["cat_ready"], m + 1)
                    need(pe, S["pT_copied2"], min(m + 3, ITEMS) if isinstance(m, int) else m + 3)
                    if not has(4):
                        need(pe, S["y_added"], m)
                    for ch in range(4):
                        for k, w in enumerate((w_hi, w_lo)):
                            at = 2 * WCOLS + ch * D
                            t = nc.tensor.matmul(bank[6][:, 0:D], cat_q[:, (j - 6) % 2, ch, :], w[:, part, at:at + D],
                                                 start=(ch == 0 and k == 0), stop=(ch == 3 and k == 1))
                    t.then_inc(S["out_proj"], 1)
                if has(2):
                    m = n - 2
                    need(pe, S["shifted2"], m)
                    need(pe, S["ev_b"], m + 1)
                    for i, t_in in enumerate((t_self, t_cross)):
                        for h in range(2):
                            at = (2 * i + h) * P
                            t = nc.tensor.matmul(bank[5][:, at:at + P], t_in[:, h, :], t_in[:, 2, :], start=True, stop=True)
                    t.then_inc(S["scores2"], 1)

            group_slots(pe, slot2)

            pe.wait_ge(S["norm_a"], ITEMS)
            pe.wait_ge(S["norm_b"], ITEMS)
            with pe.Fori(0, B) as b:
                pe.wait_ge(S["x2_ready"], b + 1)
                for c in range(C):
                    t = nc.tensor.transpose(bank[0][:, c * P:(c + 1) * P], x2_t[:, c * P:(c + 1) * P], ident)
                t.then_inc(S["x2_turned"], 1)
                pe.wait_ge(S["x2T_ready"], b + 1)
                for c in range(C):
                    t = nc.tensor.matmul(bank[1][:, 0:E], x2T_t[:, c, :], gate[:, c, :], start=(c == 0), stop=(c == C - 1))
                t.then_inc(S["router"], 1)
                pe.wait_ge(S["logits_in"], b + 1)
            pe.wait_ge(S["x2_hi"], B)
            pe.wait_ge(S["x2_lo"], B)
            x2p = (xq[:, 0:C, :], xq[:, C:2 * C, :])
            hp = hidden_parts()

            def slot3(m, j, e0):
                par = (j // 2) % 2
                tb = (j % 2) * 512
                for ic in range(IC):
                    if live(m, 2 * E):
                        if ic == 0 and j % 2 == 0:
                            e = e0 + j // 2
                            pe.wait_ge(S["w_hi_done"], WPIECES * (G + e + 1))
                            pe.wait_ge(S["w_lo_done"], WPIECES * (G + e + 1))
                        for k, free in ((0, "silu_done"), (1, "h_ready")):
                            need(pe, S[free], 4 * m + ic - 1)
                            to = bank[2 * k + ic % 2][:, :]
                            parts = [(c, a, w) for c in range(C) for a, w in ((0, w_hi), (0, w_lo), (1, w_hi))]
                            for i, (c, a, w) in enumerate(parts):
                                at = c * WCOLS + k * I + ic * P
                                t = nc.tensor.matmul(to, w[:, par, at:at + P], x2p[a][:, c, tb:tb + 512],
                                                     start=(i == 0), stop=(i == len(parts) - 1))
                        t.then_inc(S["gate_up"], 1)
                    if live(m - 1, 2 * E):
                        q, wp = (j - 1) % 2, ((j - 1) // 2) % 2
                        if ic == 0:
                            need(pe, S["h_hi"], 4 * m)
                            need(pe, S["h_lo"], 4 * m)
                        need(pe, S["acc_added"], 4 * (m - 2) + ic + 1)
                        parts = [(i, a, w) for i in range(IC) for a, w in ((0, w_hi), (0, w_lo), (1, w_hi))]
                        for k, (i, a, w) in enumerate(parts):
                            at = C * WCOLS + i * D
                            t = nc.tensor.matmul(bank[4 + ic][:, 0:D], hp[q][a][:, i, ic * L:(ic + 1) * L], w[:, wp, at:at + D],
                                                 start=(k == 0), stop=(k == len(parts) - 1))
                        t.then_inc(S["down_done"], 1)

            expert_slots(pe, slot3)

        @block.scalar
        def _(act):
            def high_piece(g, par, k, ready, count):
                act.wait_ge(S[ready], count)
                nc.scalar.activation(w_hi[:, par, k * WCOLS:(k + 1) * WCOLS], raw[:, k * WCOLS:(k + 1) * WCOLS],
                                     ACT.Copy).then_inc(S["w_hi_done"], 1)

            for c, src in enumerate((x1_all[:, 0:B * L], y_all[:, :, :].rearrange("p b d -> p (b d)")[:, 0:B * L])):
                act.wait_ge(S["ctx_in"], 32)
                nc.scalar.activation(ctx_hl[:, 0, c, :], src, ACT.Copy).then_inc(S["ctx_hi"], 1)
            for k in range(WPIECES):
                high_piece(0, 0, k, "w_scaled", k + 1)

            def exp_bank(m, j):
                need(act, S["shifted1"], 4 * m + j + 1)
                nc.scalar.activation(p_sb[:, j, :], p_sb[:, j, :], ACT.Exp, scale=HD1 ** -0.5).then_inc(S["exp1"], 1)

            def copy_turned(m, j):
                need(act, S["pT_done1"], 4 * m + j + 1)
                if j == 0:
                    need(act, S["pv_done1"], m)
                nc.scalar.activation(pT1[:, j, :], bank[4 + j % 2][:, :], ACT.Copy).then_inc(S["pT_copied1"], 1)

            def slot1(n):
                a, b, z = n - 1, n - 2, n - 3
                if live(z, B):
                    need(act, S["zT_done"], z + 1)
                    need(act, S["q_c"], z)
                    for c in range(C):
                        t = nc.scalar.activation(lnT[:, c, :], bank[7][:, c * P:(c + 1) * P], ACT.Identity,
                                                 scale=col["ln_w"][:, c:c + 1], bias=col["ln_b"][:, c:c + 1])
                    t.then_inc(S["zT_copied"], 1)
                if live(n, B):
                    if isinstance(n, int) and n == 0:
                        act.wait_ge(S["small_in"], 16)
                    need(act, S["qkv_done"], n + 1)
                    need(act, S["v_ready"], n)
                    need(act, S["turned1"], n)
                    nc.scalar.activation(qkv_raw[:, :], bank[0][:, 0:QKV1], ACT.Copy).then_inc(S["qkv_copied"], 1)
                if live(a, B):
                    exp_bank(a, 0)
                    exp_bank(a, 1)
                if live(b, B):
                    need(act, S["oT_done"], b + 1)
                    need(act, S["attn_done"], b)
                    nc.scalar.activation(oT_sb[:, :, :].rearrange("p c l -> p (c l)"), bank[7][:, 0:D], ACT.Copy).then_inc(S["oT_copied"], 1)
                if live(a, B):
                    exp_bank(a, 2)
                    copy_turned(a, 0)
                    exp_bank(a, 3)
                if live(n, B):
                    need(act, S["turned1"], n + 1)
                    need(act, S["scores1"], 4 * n)
                    nc.scalar.activation(qT1[:, :, :].rearrange("p c l -> p (c l)"), bank[1][:, 0:D], ACT.Copy).then_inc(S["qT_ready"], 1)
                if live(a, B):
                    copy_turned(a, 1)
                    copy_turned(a, 2)
                    copy_turned(a, 3)

            attention_slots(act, slot1)

            def slot2(n, j, g0):
                def has(k):
                    return live(n - k, ITEMS)

                if has(3):
                    m = n - 3
                    need(act, S["shifted2"], m + 1)
                    nc.scalar.activation(p_sb[:, (j - 3) % 4, :], p_sb[:, (j - 3) % 4, :], ACT.Exp, scale=DH ** -0.5).then_inc(S["exp2"], 1)

                def turned_qk(m, dst, at, turned, done):
                    need(act, S[turned], m + 1)
                    need(act, S["scores2"], m)
                    nc.scalar.activation(dst[:, 0:2, :].rearrange("p c l -> p (c l)"), bank[4][:, 0:2 * P], ACT.Identity,
                                         scale=col["qk_ln"][:, at:at + 1], bias=col["qk_ln"][:, at + 1:at + 2])
                    nc.scalar.activation(dst[:, 2, :], bank[4][:, 2 * P:3 * P], ACT.Identity,
                                         scale=col["qk_ln"][:, at + 2:at + 3], bias=col["qk_ln"][:, at + 3:at + 4]).then_inc(S[done], 1)

                if has(2):
                    turned_qk(n - 2, t_self, 0, "turn_a", "ev_a")
                if has(4):
                    m = n - 4
                    need(act, S["pT_done2"], m + 1)
                    need(act, S["pv_done2"], m)
                    nc.scalar.activation(pT2[:, :], bank[6][:, :], ACT.Copy).then_inc(S["pT_copied2"], 1)
                if has(2):
                    turned_qk(n - 2, t_cross, 4, "turn_b", "ev_b")
                if has(1):
                    m = n - 1
                    part_b = bank[2 * ((j - 1) % 2) + 1]
                    need(act, S["nb_ready"], m + 1)
                    need(act, S["turn_b"], m)
                    need(act, S["pv_done2"], m - 3)
                    nc.scalar.activation(v_ring[:, (j - 1) % 4, 1, :], part_b[:, 3 * DH:4 * DH], ACT.Copy)
                    for i in range(3):
                        t = nc.scalar.activation(z_cross[:, i, :], part_b[:, i * DH:(i + 1) * DH], ACT.Identity,
                                                 scale=rstd6[:, 3 + i:4 + i], bias=nb6[:, 3 + i:4 + i])
                    t.then_inc(S["norm_b"], 1)
                if has(4):
                    m = n - 4
                    part = ((j - 4) // B) % 2
                    need(act, S["pv_done2"], m + 1)
                    need(act, S["cat_m"], m)
                    for ch in range(4):
                        t = nc.scalar.activation(c_raw[:, ch * L:(ch + 1) * L], bank[7][:, ch * L:(ch + 1) * L], ACT.Copy,
                                                 scale=inv_smooth[:, part, ch:ch + 1])
                    t.then_inc(S["cat_raw"], 1)
                if 4 <= j % B < 4 + WPIECES and has(0):
                    g = g0 + j // B + 1
                    k = j % B - 4
                    need(act, S["proj_b" if k < C else "out_proj"], (g - 1) * B)
                    high_piece(g, (j // B + 1) % 2, k, "w_scaled", g * WPIECES + k + 1)

            group_slots(act, slot2)

            with act.Fori(0, B) as b:
                act.wait_ge(S["x2_turned"], b + 1)
                nc.scalar.activation(x2T_t[:, :, :].rearrange("p c l -> p (c l)"), bank[0][:, 0:D], ACT.Copy).then_inc(S["x2T_ready"], 1)
                act.wait_ge(S["x2T_ready"], b + 1)
                nc.scalar.activation(xq[:, 0:C, ds(b * L, L)], x2T_t[:, :, :], ACT.Copy).then_inc(S["x2_hi"], 1)
                act.wait_ge(S["router"], b + 1)
                nc.scalar.activation(logits[:, ds(b * E, E)], bank[1][:, 0:E], ACT.Copy).then_inc(S["logits_in"], 1)
                act.wait_ge(S["x2_lo"], b + 1)
            act.wait_ge(S["route_c"], 1)
            nc.scalar.activation(rt[:, 1, :], rt[:, 0, :], ACT.Exp).then_inc(S["comb_ready"], 1)
            hp = hidden_parts()

            def slot3(m, j, e0):
                if not live(m, 2 * E):
                    return
                for ic in range(IC):
                    need(act, S["gate_up"], 4 * m + ic + 1)
                    need(act, S["h_ready"], 4 * m + ic - 1)
                    nc.scalar.activation(s_sb[:, ic % 2, :], bank[ic % 2][:, :], ACT.Silu).then_inc(S["silu_done"], 1)
                    need(act, S["h_ready"], 4 * m + ic + 1)
                    if ic == 0:
                        need(act, S["down_done"], 4 * (m - 1))
                    nc.scalar.activation(hp[j % 2][0][:, ic, :], h_sb[:, ic % 2, :], ACT.Copy).then_inc(S["h_hi"], 1)
                if j % 2 == 1:
                    e1 = e0 + j // 2 + 1
                    if isinstance(e1, int) and e1 == E:
                        return
                    for k in range(WPIECES):
                        need(act, S["down_done"], 4 * (m - 1))
                        need(act, S["out_proj"], ITEMS)
                        high_piece(e1, (j // 2 + 1) % 2, k, "w_in", 16 * (G + e1 + 1))

            expert_slots_split(act, slot3)

        @block.gpsimd
        def _(pool):
            nc.gpsimd.memset(one16[:, :], 1.0)
            nc.gpsimd.memset(neg_half[:, :], -0.5).then_inc(S["neg_ready"], 1)
            nc.gpsimd.memset(v_one[:, HD1:HD1 + 1], 1.0).then_inc(S["v_ones"], 1)
            pool.wait_ge(S["neg_ready"], 1)
            for c, src in enumerate((x1_all[:, 0:B * L], y_all[:, :, :].rearrange("p b d -> p (b d)")[:, 0:B * L])):
                pool.wait_ge(S["ctx_hi"], c + 1)
                pool.wait_ge(S["ctx_in"], 32)
                nc.gpsimd.tensor_tensor(ctx_hl[:, 1, c, :], src, ctx_hl[:, 0, c, :].bitcast(F32), ALU.subtract).then_inc(S["ctx_lo"], 1)

            def low_piece(par, k, count):
                pool.wait_ge(S["w_hi_done"], count)
                a, b = k * WCOLS, (k + 1) * WCOLS
                nc.gpsimd.tensor_tensor(w_lo[:, par, a:b], raw[:, a:b], w_hi[:, par, a:b].bitcast(F32),
                                        ALU.subtract).then_inc(S["w_lo_done"], 1)

            for k in range(WPIECES):
                low_piece(0, k, k + 1)

            def rsqrt(var, to, ready, done, count):
                pool.wait_ge(S[ready], count)
                nc.gpsimd.tensor_tensor(to, var, neg_half[:, 0:1], ALU.pow).then_inc(S[done], 1)

            def slot1(n):
                a, b, z = n - 1, n - 2, n - 3
                if live(b, B):
                    if isinstance(b, int) and b == 0:
                        pool.wait_ge(S["x_in"], 16)
                        pool.wait_ge(S["small_in"], 16)
                    need(pool, S["ax_ready"], b)
                    nc.gpsimd.tensor_tensor(xb[:, :], x_all[:, ds(b * D, D)], col["bo"], ALU.add).then_inc(S["xb_ready"], 1)
                if live(z, B):
                    need(pool, S["quant_ready"], z + 1)
                    nc.gpsimd.tensor_tensor(q_p[:, :], q_y[:, :], q_m[:, :], ALU.add).then_inc(S["qp_c"], 1)
                    need(pool, S["qp_c"], z + 1)
                    nc.gpsimd.tensor_tensor(xq[:, :, ds(z * L, L)], q_p[:, :].rearrange("p (v l) -> p v l", l=L),
                                            q_m[:, :].rearrange("p (v l) -> p v l", l=L), ALU.subtract).then_inc(S["xq_done"], 1)
                if live(b, B):
                    for k in range(2):
                        rsqrt(ve[:, :], rstd[:, :], "var_ready", "rstd_ready", 2 * b + k + 1)
                if live(n, B):
                    need(pool, S["qkv_copied"], n + 1)
                    need(pool, S["pv_done1"], n)
                    nc.gpsimd.tensor_tensor(v_one[:, 0:HD1], qkv_raw[:, D + HD1:QKV1], one16[:, :], ALU.mult).then_inc(S["v_ready"], 1)

            attention_slots(pool, slot1)

            def slot2(n, j, g0):
                def has(k):
                    return live(n - k, ITEMS)

                if has(5):
                    m = n - 5
                    need(pool, S["cat_m"], m + 1)
                    nc.gpsimd.tensor_tensor(c_p[:, :], c_y[:, :], c_m[:, :], ALU.add).then_inc(S["cp_c"], 1)
                    need(pool, S["cp_c"], m + 1)
                    need(pool, S["out_proj"], m - 1)
                    nc.gpsimd.tensor_tensor(cat_q[:, (j - 5) % 2, :, :].rearrange("p c l -> p (c l)"), c_p[:, :], c_m[:, :],
                                            ALU.subtract).then_inc(S["cat_ready"], 1)
                if has(1):
                    m = n - 1
                    need(pool, S["var2"], m + 1)
                    need(pool, S["norm_a"], m)
                    need(pool, S["norm_b"], m)
                    nc.gpsimd.tensor_tensor(rstd6[:, :], ag[:, 3, :], neg_half[:, 0:6], ALU.pow).then_inc(S["rstd2"], 1)
                if has(3):
                    m = n - 3
                    need(pool, S["exp2"], m + 1)
                    need(pool, S["rden_ready"], m + 1)
                    p = p_sb[:, (j - 3) % 4, :].rearrange("p (h t) -> p h t", h=4)
                    nc.gpsimd.tensor_tensor(p, p, rden2[:, (j - 3) % 4, :].unsqueeze(2).broadcast_to([P, 4, P]), ALU.mult).then_inc(S["probs_ready"], 1)
                if 4 <= j % B < 4 + WPIECES and has(0):
                    g = g0 + j // B + 1
                    k = j % B - 4
                    low_piece((j // B + 1) % 2, k, g * WPIECES + k + 1)

            group_slots(pool, slot2)

            with pool.Fori(0, B) as b:
                pool.wait_ge(S["x2_var"], b + 1)
                nc.gpsimd.tensor_tensor(rstd[:, :], ve[:, :], neg_half[:, 0:1], ALU.pow).then_inc(S["x2_rstd"], 1)
                pool.wait_ge(S["x2_ready"], b + 1)
                nc.gpsimd.tensor_copy(x1_all[:, ds(b * D, D)], x2_t[:, :]).then_inc(S["x2_kept"], 1)
                pool.wait_ge(S["x2_hi"], b + 1)
                nc.gpsimd.tensor_tensor(xq[:, C:2 * C, ds(b * L, L)], x2T_t[:, :, :], xq[:, 0:C, ds(b * L, L)].bitcast(F32),
                                        ALU.subtract).then_inc(S["x2_lo"], 1)
            hp = hidden_parts()

            def slot3(m, j, e0):
                if not live(m, 2 * E):
                    return
                for ic in range(IC):
                    need(pool, S["h_hi"], 4 * m + ic + 1)
                    if ic == 0:
                        need(pool, S["down_done"], 4 * (m - 1))
                    nc.gpsimd.tensor_tensor(hp[j % 2][1][:, ic, :], h_sb[:, ic % 2, :], hp[j % 2][0][:, ic, :].bitcast(F32),
                                            ALU.subtract).then_inc(S["h_lo"], 1)
                if j % 2 == 1:
                    e1 = e0 + j // 2 + 1
                    if isinstance(e1, int) and e1 == E:
                        return
                    for k in range(WPIECES):
                        low_piece((j // 2 + 1) % 2, k, (G + e1) * WPIECES + k + 1)

            expert_slots_split(pool, slot3)

            with pool.Fori(0, B) as b:
                pool.wait_ge(S["f_var"], b + 1)
                nc.gpsimd.tensor_tensor(rstd[:, :], ve[:, :], neg_half[:, 0:1], ALU.pow).then_inc(S["f_rstd"], 1)

        @block.vector
        def _(dve):
            v = nc.vector
            dve.wait_ge(S["small_in"], 16)
            start = Chain(dve, S["consts"], 8, 0)
            v.tensor_copy(mask_b[:, :].rearrange("p (h t) -> p h t", h=4), col["mask"].unsqueeze(1).broadcast_to([P, 4, P])).then_inc(S["mask_ready"], 1)
            v.tensor_copy(ident_b[:, :], col["ident"]).then_inc(S["mask_ready"], 1)
            v.reciprocal(inv_in[:, :], col["in_scale"])
            start(v.memset(w_mul[:, G, :], 1.0))
            for c in range(C):
                t = v.tensor_tensor(w_mul[:, 0, c * NVAR:(c + 1) * NVAR], col["in_scale"][:, c * NVAR:(c + 1) * NVAR],
                                    col["w_scale"], ALU.mult)
            start(v.tensor_tensor(proj_c[:, :], col["proj"][:, 0:1], col["proj"][:, 1:2], ALU.mult))
            start(v.tensor_copy(w_mul[:, 1:G, :], w_mul[:, 0, :].unsqueeze(1).broadcast_to([P, G - 1, C * NVAR])))

            def scale_piece(g, par, k):
                dve.wait_ge(S["w_in"], 16 * (g + 1))
                if k < C:
                    for var, at, w in ((0, 0, 256), (1, 256, 128), (2, 384, 128), (3, 512, 256)):
                        a = k * WCOLS + at
                        c = k * NVAR + var
                        mul = w_mul[:, :, :].rearrange("p g c -> p (g c)")[:, ds(g * C * NVAR + c, 1)]
                        t = v.tensor_scalar(raw[:, a:a + w], raw[:, a:a + w], mul, None, ALU.mult)
                    t.then_inc(S["w_scaled"], 1)
                else:
                    v.reciprocal(inv_smooth[:, par, :], raw[:, WPIECES * WCOLS:WALL]).then_inc(S["w_scaled"], 1)

            for k in range(WPIECES):
                scale_piece(0, 0, k)

            def layer_norm(m, k, src, dst, done):
                chain = Chain(dve, S["ln_c"], 5, m)
                chain.k = 3 * k
                chain(v.bn_stats(bn[:, :], src), settle)
                chain(v.bn_aggr(mv[:, :], bn[:, :]))
                v.tensor_scalar(ve[:, :], mv[:, 1:2], EPS, None, ALU.add).then_inc(S["var_ready"], 1)
                dve.wait_ge(S["rstd_ready"], 2 * m + k + 1)
                t = v.tensor_scalar(dst, src, mv[:, 0:1], rstd[:, 0:1], ALU.subtract, ALU.mult)
                if done:
                    t.then_inc(S[done], 1)
                else:
                    chain(t, settle)

            def shift_bank(m, j):
                need(dve, S["scores1"], 4 * m + j + 1)
                s = bank[2 + j % 2][:, :].rearrange("p (h t) -> p h t", h=4)
                v.tensor_reduce(mx1[:, j, :], s, AX, ALU.max).then_inc(S["max1"], 1)
                dve.wait_ge(S["max1"], 4 * m + j + 1)
                need(dve, S["pT_done1"], 4 * (m - 1) + j + 1)
                v.tensor_tensor(p_sb[:, j, :].rearrange("p (h t) -> p h t", h=4), s,
                                mx1[:, j, :].unsqueeze(2).broadcast_to([P, 4, P]), ALU.subtract).then_inc(S["shifted1"], 1)

            cos, sin = (col[k].unsqueeze(1).broadcast_to([P, 17, ROT]) for k in ("cos", "sin"))
            heads = qkv_raw[:, 0:D + HD1].rearrange("p (h d) -> p h d", d=HD1)

            def slot1(n):
                a, b, z = n - 1, n - 2, n - 3
                if live(b, B):
                    need(dve, S["pv_done1"], b + 1)
                    need(dve, S["oT_done"], b)
                    o = bank[6][:, 0:17 * H1].rearrange("p (h d) -> p h d", d=17)
                    v.reciprocal(rden1[:, :], o[:, :, 16]).then_inc(S["rden_c"], 1)
                    dve.wait_ge(S["rden_c"], b + 1)
                    v.tensor_tensor(o_sb[:, :].rearrange("p (h d) -> p h d", d=HD1), o[:, :, 0:HD1],
                                    rden1[:, :].unsqueeze(2).broadcast_to([P, H1, HD1]), ALU.mult).then_inc(S["o_ready"], 1)
                if live(n, B):
                    need(dve, S["qkv_copied"], n + 1)
                    x1, x2 = heads[:, :, 0:ROT], heads[:, :, ROT:2 * ROT]
                    link = Chain(dve, S["rope_c"], 2, n)
                    v.tensor_tensor(rope_t[:, 0], x1, cos, ALU.mult)
                    v.tensor_tensor(rope_t[:, 1], x2, sin, ALU.mult)
                    v.tensor_tensor(rope_t[:, 2], x1, sin, ALU.mult)
                    link(v.tensor_tensor(rope_t[:, 3], x2, cos, ALU.mult))
                    v.tensor_tensor(x1, rope_t[:, 0], rope_t[:, 1], ALU.subtract)
                    link(v.tensor_tensor(x2, rope_t[:, 2], rope_t[:, 3], ALU.add))
                    v.tensor_copy(k_rep[:, :, :], qkv_raw[:, D:D + HD1].unsqueeze(1).broadcast_to([P, 8, HD1])).then_inc(S["roped"], 1)
                if live(a, B):
                    shift_bank(a, 0)
                    shift_bank(a, 1)
                    shift_bank(a, 2)
                if live(z, B):
                    need(dve, S["zT_copied"], z + 1)
                    need(dve, S["xq_done"], z)
                    y3 = q_y[:, :].rearrange("p (c v l) -> p c v l", c=C, v=NVAR)
                    v.tensor_tensor(y3, lnT[:, :, :].unsqueeze(2).broadcast_to([P, C, NVAR, L]),
                                    inv_in[:, :].rearrange("p (c v) -> p c v", c=C).unsqueeze(3).broadcast_to([P, C, NVAR, L]),
                                    ALU.mult).then_inc(S["q_c"], 1)
                    dve.wait_ge(S["q_c"], z + 1)
                    v.tensor_scalar(q_y[:, :], q_y[:, :], FP8_MAX, -FP8_MAX, ALU.min, ALU.max).then_inc(S["cq_c"], 1)
                    dve.wait_ge(S["cq_c"], z + 1)
                    v.tensor_scalar(q_m[:, :].bitcast(U16), q_y[:, :].bitcast(U16), NO_SIGN, None, ALU.bitwise_and).then_inc(S["abs_c"], 1)
                    dve.wait_ge(S["abs_c"], z + 1)
                    v.tensor_scalar(q_m[:, :], q_m[:, :], FP8_MIN_EXP, FP8_SHIFT, ALU.max, ALU.mult).then_inc(S["quant_ready"], 1)
                if live(a, B):
                    shift_bank(a, 3)
                if live(n, B):
                    need(dve, S["turned1"], n + 1)
                    need(dve, S["qT_ready"], n + 1)
                    need(dve, S["scores1"], 4 * n)
                    v.tensor_tensor(k_bd[:, :, :], bank[1][:, D:D + P].unsqueeze(1).broadcast_to([P, 8, L]),
                                    col["head"].unsqueeze(2).broadcast_to([P, 8, L]), ALU.mult).then_inc(S["kbd_ready"], 1)
                if live(b, B):
                    need(dve, S["attn_done"], b + 1)
                    need(dve, S["xb_ready"], b + 1)
                    need(dve, S["zT_done"], b)
                    need(dve, S["z2_ready"], b)
                    v.tensor_tensor(ax[:, :], bank[7][:, 0:D], xb[:, :], ALU.add).then_inc(S["ax_ready"], 1)
                    dve.wait_ge(S["ax_ready"], b + 1)
                    if isinstance(b, int) and b == 0:
                        dve.wait_ge(S["ctx_lo"], C)
                    x1 = x1_all[:, ds(b * D, D)]
                    layer_norm(b, 0, ax[:, :], x1, None)
                    layer_norm(b, 1, x1, z2[:, :], "z2_ready")

            attention_slots(dve, slot1)

            def slot2(n, j, g0):
                def has(k):
                    return live(n - k, ITEMS)

                if has(7):
                    m = n - 7
                    b = (j - 7) % B
                    need(dve, S["out_proj"], m + 1)
                    if isinstance(m, int) and m < B:
                        v.tensor_copy(y_all[:, b, :], bank[6][:, 0:D]).then_inc(S["y_added"], 1)
                    else:
                        need(dve, S["y_added"], m - B + 1)
                        v.tensor_tensor(y_all[:, b, :], bank[6][:, 0:D], y_all[:, b, :], ALU.add).then_inc(S["y_added"], 1)
                if has(3):
                    m = n - 3
                    need(dve, S["scores2"], m + 1)
                    need(dve, S["pT_done2"], m - 3)
                    s = bank[5][:, :].rearrange("p (h t) -> p h t", h=4)
                    v.tensor_reduce(mx2[:, (j - 3) % 4, :], s, AX, ALU.max).then_inc(S["max2"], 1)
                    dve.wait_ge(S["max2"], m + 1)
                    v.tensor_tensor(p_sb[:, (j - 3) % 4, :].rearrange("p (h t) -> p h t", h=4), s,
                                    mx2[:, (j - 3) % 4, :].unsqueeze(2).broadcast_to([P, 4, P]), ALU.subtract).then_inc(S["shifted2"], 1)
                if has(1):
                    m = n - 1
                    part_a, part_b = bank[2 * ((j - 1) % 2)], bank[2 * ((j - 1) % 2) + 1]
                    link = Chain(dve, S["agg_c"], 4, m)
                    need(dve, S["proj_a"], m + 1)
                    need(dve, S["nb_ready"], m)
                    for i in range(3):
                        v.bn_stats(st[:, i, :], part_a[:, i * DH:(i + 1) * DH])
                    need(dve, S["proj_b"], m + 1)
                    for i in range(3):
                        t = v.bn_stats(st[:, 3 + i, :], part_b[:, i * DH:(i + 1) * DH])
                    link(t)
                    need(dve, S["rstd2"], m)
                    v.tensor_tensor(sum_m2[:, :, :], st[:, :, 1:3], st[:, :, 4:6], ALU.add)
                    link(v.tensor_tensor(ag[:, 0, :], st[:, :, 1], st[:, :, 4], ALU.subtract))
                    link(v.scalar_tensor_tensor(out=ag[:, 1, :], in0=ag[:, 0, :], scalar=DH / 4, in1=ag[:, 0, :],
                                                op0=ALU.mult, op1=ALU.mult))
                    need(dve, S["norm_a"], m)
                    v.tensor_scalar(mean6[:, :], sum_m2[:, :, 0], 0.5, None, ALU.mult)
                    link(v.tensor_tensor(ag[:, 2, :], ag[:, 1, :], sum_m2[:, :, 1], ALU.add))
                    v.tensor_scalar(ag[:, 3, :], ag[:, 2, :], 1.0 / DH, EPS, ALU.mult, ALU.add).then_inc(S["var2"], 1)
                if has(5):
                    m = n - 5
                    need(dve, S["cat_raw"], m + 1)
                    need(dve, S["cat_ready"], m)
                    v.tensor_scalar(c_y[:, :], c_raw[:, :], FP8_MAX, -FP8_MAX, ALU.min, ALU.max).then_inc(S["cq_c"], 1)
                    dve.wait_ge(S["cq_c"], B + m + 1)
                    v.tensor_scalar(c_m[:, :].bitcast(U16), c_y[:, :].bitcast(U16), NO_SIGN, None, ALU.bitwise_and).then_inc(S["abs_c"], 1)
                    dve.wait_ge(S["abs_c"], B + m + 1)
                    v.tensor_scalar(c_m[:, :], c_m[:, :], FP8_MIN_EXP, FP8_SHIFT, ALU.max, ALU.mult).then_inc(S["cat_m"], 1)
                if has(3):
                    m = n - 3
                    need(dve, S["exp2"], m + 1)
                    v.tensor_reduce(sums[:, (j - 3) % 4, :], p_sb[:, (j - 3) % 4, :].rearrange("p (h t) -> p h t", h=4), AX, ALU.add).then_inc(S["sum_c"], 1)
                    dve.wait_ge(S["sum_c"], m + 1)
                    need(dve, S["probs_ready"], m - 3)
                    v.reciprocal(rden2[:, (j - 3) % 4, :], sums[:, (j - 3) % 4, :]).then_inc(S["rden_ready"], 1)
                if has(1):
                    m = n - 1
                    need(dve, S["pv_done2"], m - 3)
                    v.tensor_copy(v_ring[:, (j - 1) % 4, 0, :], part_a[:, 3 * DH:4 * DH])
                    need(dve, S["rstd2"], m + 1)
                    need(dve, S["norm_b"], m)
                    v.scalar_tensor_tensor(out=nb6[:, :], in0=sum_m2[:, :, 0], scalar=-0.5, in1=rstd6[:, :],
                                           op0=ALU.mult, op1=ALU.mult).then_inc(S["nb_ready"], 1)
                    need(dve, S["turn_a"], m)
                    for i in range(3):
                        t = v.tensor_scalar(z_self[:, i, :], part_a[:, i * DH:(i + 1) * DH], mean6[:, i:i + 1],
                                            rstd6[:, i:i + 1], ALU.subtract, ALU.mult)
                    t.then_inc(S["norm_a"], 1)
                if 4 <= j % B < 4 + WPIECES and has(0):
                    g = g0 + j // B + 1
                    k = j % B - 4
                    if k == 2:
                        need(dve, S["cat_raw"], (g - 1) * B)
                    scale_piece(g, (j // B + 1) % 2, k)

            group_slots(dve, slot2)

            y_flat = y_all[:, :, :].rearrange("p b d -> p (b d)")
            with dve.Fori(0, B) as b:
                if True:
                    dve.wait_ge(S["y_added"], ITEMS)
                    link = Chain(dve, S["x2_c"], 3, b)
                    link(v.scalar_tensor_tensor(out=ax[:, :], in0=y_flat[:, ds(b * D, D)], scalar=proj_c[:, 0:1],
                                                in1=x1_all[:, ds(b * D, D)], op0=ALU.mult, op1=ALU.add))
                    link(v.bn_stats(bn[:, :], ax[:, :]), settle)
                    link(v.bn_aggr(mv[:, :], bn[:, :]))
                    v.tensor_scalar(ve[:, :], mv[:, 1:2], EPS, None, ALU.add).then_inc(S["x2_var"], 1)
                    dve.wait_ge(S["x2_rstd"], b + 1)
                    v.tensor_scalar(x2_t[:, :], ax[:, :], mv[:, 0:1], rstd[:, 0:1], ALU.subtract, ALU.mult).then_inc(S["x2_ready"], 1)
                    dve.wait_ge(S["x2_turned"], b + 1)
                    dve.wait_ge(S["x2_kept"], b + 1)

            dve.wait_ge(S["logits_in"], B)
            RC = Chain(dve, S["f_c"], 1000, 0)

            def be(i):
                return rt[:, i, :].rearrange("p (b e) -> p b e", b=B)

            def spread(i):
                return r1[:, i, :].unsqueeze(2).broadcast_to([P, B, E])

            lg = logits[:, :].rearrange("p (b e) -> p b e", b=B)
            rank = col["rank"].unsqueeze(1).broadcast_to([P, B, E])
            RC(v.tensor_reduce(r1[:, 0, :], lg, AX, ALU.max))
            v.tensor_tensor(be(0), lg, spread(0), ALU.subtract).then_inc(S["route_c"], 1)
            dve.wait_ge(S["comb_ready"], 1)
            RC(v.tensor_reduce(r1[:, 1, :], be(1), AX, ALU.add))
            RC(v.reciprocal(r1[:, 2, :], r1[:, 1, :]))
            RC(v.tensor_tensor(be(2), be(1), spread(2), ALU.mult))
            RC(v.memset(be(7), 0.0))
            for top in range(2):
                RC(v.tensor_reduce(r1[:, 3, :], be(2), AX, ALU.max))
                RC(v.tensor_tensor(be(3), be(2), spread(3), ALU.is_equal))
                RC(v.tensor_tensor(be(4), be(3), rank, ALU.mult))
                RC(v.tensor_reduce(r1[:, 4, :], be(4), AX, ALU.max))
                RC(v.tensor_tensor(be(5), be(4), spread(4), ALU.is_equal))
                RC(v.tensor_tensor(be(6), be(5), be(2), ALU.mult))
                RC(v.tensor_tensor(be(7), be(7), be(6), ALU.add))
                RC(v.scalar_tensor_tensor(out=rt[:, 2, :], in0=rt[:, 5, :], scalar=-2.0, in1=rt[:, 2, :], op0=ALU.mult, op1=ALU.add))
            RC(v.tensor_reduce(r1[:, 0, :], be(7), AX, ALU.add))
            RC(v.reciprocal(r1[:, 1, :], r1[:, 0, :]))
            RC(v.tensor_tensor(comb[:, :, :], be(7), spread(1), ALU.mult))
            routed = RC.k

            comb_f = comb[:, :, :].rearrange("p b e -> p (b e)")

            def slot3(m, j, e0):
                for ic in range(IC):
                    if live(m, 2 * E):
                        need(dve, S["silu_done"], 4 * m + ic + 1)
                        need(dve, S["h_lo"], 4 * m + ic - 1)
                        need(dve, S["h_hi"], 4 * m + ic - 1)
                        v.tensor_tensor(h_sb[:, ic % 2, :], bank[2 + ic % 2][:, :], s_sb[:, ic % 2, :], ALU.mult).then_inc(S["h_ready"], 1)
                    if live(m - 1, 2 * E):
                        b = ((j - 1) % 2) * 4 + ic
                        if j == 0 and isinstance(e0, int):
                            at = b * E + e0 - 1
                        elif j == 0:
                            at = e0 + (b * E - 1)
                        else:
                            at = e0 + (b * E + (j - 1) // 2)
                        need(dve, S["down_done"], 4 * (m - 1) + ic + 1)
                        need(dve, S["acc_added"], 4 * (m - 3) + ic + 1)
                        if isinstance(m, int) and m - 1 < 2:
                            v.tensor_scalar(y_all[:, b, :], bank[4 + ic][:, 0:D], comb_f[:, at:at + 1], None,
                                            ALU.mult).then_inc(S["acc_added"], 1)
                        else:
                            v.scalar_tensor_tensor(out=y_all[:, b, :], in0=bank[4 + ic][:, 0:D], scalar=comb_f[:, ds(at, 1)],
                                                   in1=y_all[:, b, :], op0=ALU.mult, op1=ALU.add).then_inc(S["acc_added"], 1)

            expert_slots(dve, slot3)

            with dve.Fori(0, B) as b:
                dve.wait_ge(S["acc_added"], 4 * 2 * E)
                link = Chain(dve, S["x2_c"], 3, b + B)
                link(v.tensor_tensor(ax[:, :], y_flat[:, ds(b * D, D)], x1_all[:, ds(b * D, D)], ALU.add))
                link(v.bn_stats(bn[:, :], ax[:, :]), settle)
                link(v.bn_aggr(mv[:, :], bn[:, :]))
                v.tensor_scalar(ve[:, :], mv[:, 1:2], EPS, None, ALU.add).then_inc(S["f_var"], 1)
                dve.wait_ge(S["f_rstd"], b + 1)
                v.tensor_scalar(x_all[:, ds(b * D, D)], ax[:, :], mv[:, 0:1], rstd[:, 0:1], ALU.subtract, ALU.mult).then_inc(S["out_ready"], 1)
                dve.wait_ge(S["out_ready"], b + 1)


def _small(w):
    f = np.float32
    pos = np.arange(L, dtype=f)
    dims = 2 * ROT
    inv_freq = np.exp(-np.log(f(10000.0)) * (np.arange(0, dims, 2).astype(f) / f(dims)))
    theta = pos[:, None] * inv_freq[None, :]
    i, j = np.arange(L)[:, None], np.arange(L)[None, :]
    chunks = lambda a: np.asarray(a).reshape(C, P, -1).transpose(1, 0, 2).reshape(P, -1)
    spread = lambda a: np.broadcast_to(np.asarray(a).reshape(1, -1), (P, np.asarray(a).size))
    in_scale = np.stack([w[f"L0_xattn_{n}_in_scale"].reshape(C, P) for n in ("q", "k", "v", "qx")], axis=-1)
    cols = {
        "ident": np.eye(P, dtype=f),
        "mask": np.where((i - j >= 0) & (i - j < WINDOW), f(0), f(-1e9)),
        "cos": np.cos(theta), "sin": np.sin(theta),
        "head": (np.arange(P)[:, None] // HD1 == np.arange(8)[None, :]).astype(f),
        "ln_w": chunks(w["L0_xattn_ln_w"]), "ln_b": chunks(w["L0_xattn_ln_b"]),
        "in_scale": in_scale.transpose(1, 0, 2).reshape(P, C * NVAR),
        "qk_ln": np.stack([w[f"L0_xattn_{n}"] for n in ("qln_w", "qln_b", "kln_w", "kln_b", "qxln_w", "qxln_b", "kxln_w", "kxln_b")], axis=1),
        "w_scale": np.concatenate([spread(w[f"L0_xattn_{n}_scale"]) for n in ("wq", "wk", "wv", "wqx")], axis=1),
        "proj": np.concatenate([spread(w["L0_xattn_proj_w_scale"]), spread(w["L0_xattn_proj_in_scale"])], axis=1),
        "bo": spread(w["L0_attn_bo"]),
        "wqkv": chunks(np.concatenate([w["L0_attn_Wq"], w["L0_attn_Wk"], w["L0_attn_Wv"]], axis=1)),
        "wo": chunks(w["L0_attn_Wo"]),
        "gate": chunks(w["L0_ffn_gate_weight"].T),
        "rank": np.broadcast_to(np.arange(E, 0, -1).astype(f)[None], (P, E)),
    }
    return np.ascontiguousarray(np.concatenate([cols[k] for k in COL], axis=1))


def _weights(w):
    def grouped(a, per):
        return a.reshape(G, per * DH, C, P).transpose(0, 3, 2, 1)

    kx, vx = w["L0_xattn_w_kv_x"][:G * DH], w["L0_xattn_w_kv_x"][G * DH:]
    proj = np.concatenate([grouped(w["L0_xattn_wq"], 2), grouped(w["L0_xattn_wk"], 1), grouped(w["L0_xattn_wv"], 1),
                           grouped(w["L0_xattn_wqx"], 2), grouped(kx, 1), grouped(vx, 1)], axis=3).reshape(G, P, C * WCOLS)
    wp = w["L0_xattn_wproj"].T.reshape(2, G, 2, DH, D).transpose(1, 3, 0, 2, 4).reshape(G, P, 4 * D)
    smooth = w["L0_xattn_proj_smooth"].reshape(2, G, 2, DH).transpose(1, 3, 0, 2).reshape(G, P, 4)
    gu = w["L0_ffn_gate_up_proj"].reshape(E, 2 * I, C, P).transpose(0, 3, 2, 1).reshape(E, P, C * WCOLS)
    down = w["L0_ffn_down_proj"].reshape(E, D, IC, P).transpose(0, 3, 2, 1).reshape(E, P, IC * D)
    ones = np.ones((E, P, 4), np.float32)
    return np.ascontiguousarray(np.concatenate([np.concatenate([proj, wp, smooth], axis=2),
                                                np.concatenate([gu, down, ones], axis=2)], axis=0))


def kernel(**inputs):
    import concourse.bacc as _bacc
    from concourse.bass_utils import run_bass_kernel_spmd as _run

    w = {k: np.asarray(v) for k, v in inputs.items()}
    arrays = {
        "in_x": np.ascontiguousarray(w["x"]),
        "in_xT": np.ascontiguousarray(w["x"].reshape(B, L, C, P).transpose(0, 3, 2, 1)),
        "in_ctxT": np.ascontiguousarray(w["ctx_2048"].reshape(B * L, C, P).transpose(1, 2, 0)),
        "in_small": _small(w),
        "in_wall": _weights(w),
    }
    nc = _bacc.Bacc("TRN2", target_bir_lowering=False, num_devices=1)
    args = [nc.dram_tensor(k, a.shape, mybir.dt.from_np(a.dtype), kind="ExternalInput").ap() for k, a in arrays.items()]
    args.append(nc.dram_tensor("out", (B, L, D), F32, kind="ExternalOutput").ap())
    decoder_layer(nc, *args)
    r = _run(nc, [arrays], core_ids=[0])
    return r.results[0]["out"]
```

```python
from contextlib import ExitStack

import numpy as np

import concourse.bass as bass
from concourse import mybir

F32 = mybir.dt.float32
F32R = mybir.dt.float32r
BF16 = mybir.dt.bfloat16
U16 = mybir.dt.uint16
NO_SIGN = 0x7FFF
ALU = mybir.AluOpType
ACT = mybir.ActivationFunctionType
AX = mybir.AxisListType.X

P = 128
B, L, D = 8, 128, 256
C = D // P
H1, HD1 = 16, 16
ROT = HD1 // 4
WINDOW = 64
G, DH = 8, 128
E, I = 8, 512
IC = I // P
NVAR = 4
EPS = 1e-5
FP8_MAX = 448.0
FP8_MIN_EXP = 1.5 * 2.0 ** -6
FP8_SHIFT = 2.0 ** 20
QKV1 = D + 2 * HD1
WCOLS = 1024
PIECE = 512
WPIECES = 3 * WCOLS // PIECE
PROJ_PIECES = C * WCOLS // PIECE
SCALED = PROJ_PIECES + 1
WALL = WPIECES * PIECE + 4

_at = 0
COL = {}
for _name, _n in (("ident", P), ("mask", P), ("cos", ROT), ("sin", ROT), ("head", 8), ("ln_w", C), ("ln_b", C),
                  ("in_scale", C * NVAR), ("qk_ln", 8), ("w_scale", NVAR), ("proj", 2), ("wqkv", C * QKV1),
                  ("bo", D), ("wo", C * D), ("gate", C * E), ("rank", E)):
    COL[_name] = (_at, _at + _n)
    _at += _n
SMALL = _at
FIRST = COL["bo"][0]


def need(eng, sem, value):
    if isinstance(value, int) and value <= 0:
        return
    eng.wait_ge(sem, value)


class Chain:

    def __init__(self, eng, sem, per_item, item):
        self.eng, self.sem, self.per, self.base, self.k = eng, sem, per_item, item * per_item, 0

    def __call__(self, ins, settle=None):
        self.k += 1
        assert self.k <= self.per
        ins.then_inc(self.sem, 1)
        self.eng.wait_ge(self.sem, self.base + self.k)
        if settle:
            settle()


def live(item, count):
    return not isinstance(item, int) or 0 <= item < count


def decoder_layer(nc, x, xT, ctxT, small, wall, out):
    ctx = ExitStack()
    with ctx:
        def sb(name, cols, dt=F32):
            return ctx.enter_context(nc.sbuf_tensor(name, [P] + list(cols), dt))

        def sem(name):
            return ctx.enter_context(nc.semaphore(name))

        bank = [ctx.enter_context(nc.psum_tensor(f"bank{i}", [P, 512], F32)) for i in range(8)]

        sm = sb("small_sb", [SMALL])
        col = {k: sm[:, a:b] for k, (a, b) in COL.items()}
        x_all = sb("x_all", [B * D])
        x1_all = sb("x1_all", [B * D])
        y_all = sb("y_all", [B, D])
        xq = sb("xq", [C * NVAR, B * L], F32R)
        ctx_hl = sb("ctx_hl", [2, C, B * L], F32R)
        raw = sb("raw", [WALL])
        w_hi = sb("w_hi", [2, WPIECES * PIECE], F32R)
        w_lo = sb("w_lo", [2, WPIECES * PIECE], F32R)
        neg_half = sb("neg_half", [8])
        mask_b = sb("mask_b", [512], BF16)
        ident_b = sb("ident_b", [P], BF16)
        inv_in = sb("inv_in", [C * NVAR])
        w_mul = sb("w_mul", [G + 1, C * NVAR])
        inv_smooth = sb("inv_smooth", [2, 4])
        proj_c = sb("proj_c", [1])
        seen = sb("seen", [1])
        one16 = sb("one16", [HD1])
        warm = sb("warm", [1])
        xT_in = sb("xT_in", [C, L])
        qkv_raw = sb("qkv_raw", [QKV1])
        rope_t = sb("rope_t", [4, 17, ROT])
        k_rep = sb("k_rep", [8, HD1])
        v_one = sb("v_one", [B * 17])
        qT1 = sb("qT1", [C, L])
        k_bd = sb("k_bd", [8, L])
        p_sb = sb("p_sb", [4, 512])
        pT1 = sb("pT1", [4, 512])
        mx1 = sb("mx1", [4, 4])
        neg_mx1 = sb("neg_mx1", [4, 4])
        rden1 = sb("rden1", [H1])
        o_sb = sb("o_sb", [D])
        oT_sb = sb("oT_sb", [C, L])
        xb = sb("xb", [D])
        ax = sb("ax", [D])
        z2 = sb("z2", [D])
        lnT = sb("lnT", [C, L])
        bn = sb("bn", [6])
        mv = sb("mv", [2])
        ve = sb("ve", [1])
        rstd = sb("rstd", [1])
        q_y = sb("q_y", [C * NVAR * L], BF16)
        q_m = sb("q_m", [C * NVAR * L], BF16)
        q_p = sb("q_p", [C * NVAR * L])
        st = sb("st", [6, 6])
        sum_m2 = sb("sum_m2", [6, 2])
        ag = sb("ag", [4, 6])
        mean6 = sb("mean6", [6])
        rstd6 = sb("rstd6", [6])
        nb6 = sb("nb6", [6])
        z_self = sb("z_self", [3, DH])
        z_cross = sb("z_cross", [3, DH])
        t_self = sb("t_self", [3, L])
        t_cross = sb("t_cross", [3, L])
        v_ring = sb("v_ring", [4, 2, DH])
        mx2 = sb("mx2", [4])
        neg_mx = sb("neg_mx", [4])
        sums = sb("sums", [4])
        rden2 = sb("rden2", [4])
        pT2 = sb("pT2", [512])
        c_raw = sb("c_raw", [512], BF16)
        c_y = sb("c_y", [512], BF16)
        c_m = sb("c_m", [512], BF16)
        c_p = sb("c_p", [512])
        cat_q = sb("cat_q", [2, 4, L], F32R)
        x2_t = sb("x2_t", [2, D])
        x2T_t = k_bd[:, 0:2 * C, :].rearrange("p (i c) l -> p i c l", i=2)
        logits = sb("logits", [B * E])
        comb = sb("comb", [B, E])
        rt = sb("rt", [8, B * E])
        r1 = sb("r1", [6, B])
        bn8 = sb("bn8", [B, 6])
        mv8 = sb("mv8", [B, 2])
        ve8 = sb("ve8", [B])
        rstd8 = sb("rstd8", [B])
        s_sb, h_sb = pT1[:, 0:2, :], pT1[:, 2:4, :]

        S = {n: sem(n) for n in (
            "small_in more_in x_in ctx_in xT_in_s w_in out_done "
            "consts neg_ready v_ones mask_ready "
            "w_scaled w_hi_done w_lo_done ctx_hi ctx_lo "
            "qkv_done qkv_copied roped rope_c turned1 qT_ready kbd_ready scores1 max1 neg_max1 exp1 "
            "pT_done1 pT_copied1 v_ready pv_done1 rden_c o_ready oT_done oT_copied attn_done xb_ready "
            "ax_ready ln_c var_ready rstd_ready z2_ready zT_done zT_copied q_c abs_c quant_ready qp_c xq_done "
            "proj_a proj_b agg_c var2 rstd2 nb_ready norm_a norm_b turn_a turn_b ev_a ev_b scores2 max2 neg_max2 "
            "exp2 rden_ready probs_ready pT_done2 pT_copied2 pv_done2 cat_raw cq_c cat_m cp_c cat_ready "
            "out_proj y_added "
            "x2_c x2_var x2_rstd x2_ready x2_turned x2T_ready x2_hi x2_lo x2_kept router logits_in route_c "
            "comb_ready gate_up silu_done h_ready h_hi h_lo down_done acc_added "
            "f_c out_c f_var f_rstd out_ready").split()}

        block = ctx.enter_context(nc.Block())

        def settle():
            nc.vector.tensor_copy(seen[:, :], proj_c[:, :])

        def ds(start, n):
            return bass.ds(start, n)

        LAG1 = 3

        def attention_slots(eng, slot, lag=LAG1):
            for n in range(lag):
                slot(n)
            with eng.Fori(lag, B) as n:
                slot(n)
            for n in range(B, B + lag):
                slot(n)

        ITEMS = G * B
        SPAN = 2 * B
        LAG2 = 8
        X2_LAG = 3

        def group_slots(eng, slot, x2_steps):
            for j in range(SPAN):
                slot(j, j, 0)
            with eng.Fori(1, G // 2) as r:
                for j in range(SPAN):
                    slot(r * SPAN + j, j, r * 2)
            for j in range(B + X2_LAG):
                if j < LAG2:
                    slot(ITEMS + j, j, G)
                x2_steps(j)

        ESPAN = 4

        def expert_slots(eng, slot):
            for j in range(ESPAN):
                slot(j, j, 0)
            with eng.Fori(1, E // 2 - 1) as r:
                for j in range(ESPAN):
                    slot(r * ESPAN + j, j, r * 2)
            for j in range(ESPAN + 1):
                slot(2 * E - ESPAN + j, j, E - 2)

        def context():
            return x1_all[:, 0:B * L], y_all[:, :, :].rearrange("p b d -> p (b d)")[:, 0:B * L]

        def next_piece(j, ic, e1):
            k = (j % 2) * IC + ic
            return None if k >= WPIECES or (isinstance(e1, int) and e1 == E) else k

        def hidden_parts():
            a = [xq[:, (2 + k) * C:(3 + k) * C, :].rearrange("p c t -> p (c t)").rearrange("p (i t) -> p i t", i=IC) for k in range(2)]
            b = [ctx_hl[:, k, :, :].rearrange("p c t -> p (c t)").rearrange("p (i t) -> p i t", i=IC) for k in range(2)]
            return a, b

        @block.sync
        def _(sp):
            sp.dma_start(sm[:, 0:FIRST], small[:, 0:FIRST]).then_inc(S["small_in"], 16)
            sp.dma_start(xT_in[:, :, :], xT[0]).then_inc(S["xT_in_s"], 16)
            sp.dma_start(sm[:, FIRST:SMALL], small[:, FIRST:SMALL]).then_inc(S["more_in"], 16)
            sp.dma_start(x1_all[:, 0:B * L], ctxT[0]).then_inc(S["ctx_in"], 16)
            sp.dma_start(y_all[:, :, :].rearrange("p b d -> p (b d)")[:, 0:B * L], ctxT[1]).then_inc(S["ctx_in"], 16)

            sp.wait_ge(S["qkv_done"], 1)
            sp.dma_start(xT_in[:, :, :], xT[1]).then_inc(S["xT_in_s"], 16)
            sp.dma_start(raw[:, :], wall[0]).then_inc(S["w_in"], 16)
            sp.dma_start(x_all[:, :].rearrange("p (b d) -> p b d", b=B), x.rearrange("b p d -> p b d")).then_inc(S["x_in"], 16)
            with sp.Fori(2, B) as n:
                sp.wait_ge(S["qkv_done"], n)
                sp.dma_start(xT_in[:, :, :], xT[ds(n, 1)].rearrange("o p c l -> p (o c) l")).then_inc(S["xT_in_s"], 16)
            with sp.Fori(1, G + E) as g:
                sp.wait_ge(S["w_lo_done"], g * WPIECES)
                sp.wait_ge(S["w_hi_done"], g * WPIECES)
                sp.dma_start(raw[:, :], wall[ds(g, 1)].rearrange("o p c -> p (o c)")).then_inc(S["w_in"], 16)
            for b in range(0, B, 2):
                sp.wait_ge(S["out_ready"], b + 1)
                sp.dma_start(out[b], x_all[:, b * D:(b + 1) * D]).then_inc(S["out_done"], 16)
            sp.wait_ge(S["out_done"], 16 * B)

        @block.tensor
        def _(pe):
            ident = col["ident"]
            wqkv = col["wqkv"].rearrange("p (c n) -> p c n", c=C)
            wo = col["wo"].rearrange("p (c n) -> p c n", c=C)
            gate = col["gate"].rearrange("p (c e) -> p c e", c=C)

            def scores_bank(m, j):
                if j == 0:
                    need(pe, S["qT_ready"], m + 1)
                    need(pe, S["kbd_ready"], m + 1)
                need(pe, S["exp1"], 4 * m + j - 1)
                to = bank[2 + j % 2][:, :]
                nc.tensor.matmul(to, qT1[:, j // 2, :], k_bd[:, 4 * (j % 2):4 * (j % 2) + 4, :], start=True, stop=False)
                nc.tensor.matmul(to, ident_b[:, :], mask_b[:, :], start=False, stop=True).then_inc(S["scores1"], 1)

            def turn_probs(m, j):
                need(pe, S["exp1"], 4 * m + j + 1)
                need(pe, S["pT_copied1"], 4 * m + j - 1)
                for i in range(4):
                    t = nc.tensor.transpose(bank[4 + j % 2][:, i * P:(i + 1) * P], p_sb[:, j, i * P:(i + 1) * P], ident)
                t.then_inc(S["pT_done1"], 1)

            def values1(m, j):
                if j == 0:
                    need(pe, S["o_ready"], m)
                    need(pe, S["v_ready"], m + 1)
                need(pe, S["pT_copied1"], 4 * m + j + 1)
                for i in range(4):
                    h = 4 * j + i
                    t = nc.tensor.matmul(bank[6][:, h * 17:(h + 1) * 17], pT1[:, j, i * P:(i + 1) * P], v_one[:, ds(m * 17, 17)],
                                         start=True, stop=True)
                if j == 3:
                    t.then_inc(S["pv_done1"], 1)

            def slot1(n):
                a, b, z = n - 1, n - 2, n - 3
                if live(n, B):
                    if isinstance(n, int) and n == 0:
                        pe.wait_ge(S["small_in"], 16)
                        pe.wait_ge(S["mask_ready"], 2)
                    need(pe, S["xT_in_s"], 16 * (n + 1))
                    need(pe, S["qkv_copied"], n)
                    need(pe, S["zT_copied"], n - 3)
                    for c in range(C):
                        t = nc.tensor.matmul(bank[0][:, 0:QKV1], xT_in[:, c, :], wqkv[:, c, :], start=(c == 0), stop=(c == C - 1))
                    t.then_inc(S["qkv_done"], 1)
                if live(a, B):
                    scores_bank(a, 0)
                if live(b, B):
                    turn_probs(b, 2)
                if live(a, B):
                    scores_bank(a, 1)
                if live(b, B):
                    turn_probs(b, 3)
                    values1(b, 1)
                    values1(b, 2)
                    values1(b, 3)
                if live(a, B):
                    scores_bank(a, 2)
                    turn_probs(a, 0)
                if live(n, B):
                    need(pe, S["roped"], n + 1)
                    need(pe, S["kbd_ready"], n)
                    for c in range(C):
                        nc.tensor.transpose(bank[1][:, c * P:(c + 1) * P], qkv_raw[:, c * P:(c + 1) * P], ident)
                    nc.tensor.transpose(bank[1][:, D:D + P], k_rep[:, :, :].rearrange("p a b -> p (a b)"), ident).then_inc(S["turned1"], 1)
                if live(b, B):
                    need(pe, S["o_ready"], b + 1)
                    need(pe, S["ax_ready"], b)
                    for c in range(C):
                        t = nc.tensor.transpose(bank[7][:, c * P:(c + 1) * P], o_sb[:, c * P:(c + 1) * P], ident)
                    t.then_inc(S["oT_done"], 1)
                if live(a, B):
                    scores_bank(a, 3)
                if live(z, B):
                    need(pe, S["z2_ready"], z + 1)
                    need(pe, S["qkv_copied"], min(n + 1, B) if isinstance(n, int) else n + 1)
                    need(pe, S["zT_copied"], z)
                    for c in range(C):
                        t = nc.tensor.transpose(bank[0][:, c * P:(c + 1) * P], z2[:, c * P:(c + 1) * P], ident)
                    t.then_inc(S["zT_done"], 1)
                if live(a, B):
                    turn_probs(a, 1)
                if isinstance(b, int) and b == 0:
                    pe.wait_ge(S["more_in"], 16)
                if live(b, B):
                    need(pe, S["oT_copied"], b + 1)
                    for c in range(C):
                        t = nc.tensor.matmul(bank[7][:, 0:D], oT_sb[:, c, :], wo[:, c, :], start=(c == 0), stop=(c == C - 1))
                    t.then_inc(S["attn_done"], 1)
                if live(a, B):
                    values1(a, 0)

            attention_slots(pe, slot1)

            def slot2(n, j, g0):
                def has(k):
                    return live(n - k, ITEMS)

                par = (j // B) % 2
                bt = (j % B) * L
                hi, lo = w_hi[:, par, :], w_lo[:, par, :]
                bank_a, bank_b = bank[2 * (j % 2)], bank[2 * (j % 2) + 1]

                def turn_qk(m, z, src, inc, free, count):
                    need(pe, S[src], m + 1)
                    need(pe, S[free], count)
                    for i in range(3):
                        t = nc.tensor.transpose(bank[4][:, i * P:(i + 1) * P], z[:, i, :], ident)
                    t.then_inc(S[inc], 1)

                if has(2):
                    turn_qk(n - 2, z_self, "norm_a", "turn_a", "ev_b", n - 2)
                if has(0):
                    if j % B == 0:
                        g = g0 + j // B
                        pe.wait_ge(S["w_hi_done"], WPIECES * g + PROJ_PIECES)
                        pe.wait_ge(S["w_lo_done"], WPIECES * g + PROJ_PIECES)
                        if isinstance(n, int) and n == 0:
                            pe.wait_ge(S["ctx_hi"], C)
                            pe.wait_ge(S["ctx_lo"], C)
                            pe.wait_ge(S["zT_copied"], B)
                            pe.wait_ge(S["ax_ready"], B)
                    if isinstance(n, int) and n < B:
                        pe.wait_ge(S["xq_done"], n + 1)
                    need(pe, S["norm_a"], n - 1)
                    for var, at, w in ((0, 0, 256), (1, 256, 128), (2, 384, 128)):
                        for c in range(C):
                            for k, part in enumerate((hi, lo)):
                                t = nc.tensor.matmul(bank_a[:, at:at + w], xq[:, c * NVAR + var, bt:bt + L],
                                                     part[:, c * WCOLS + at:c * WCOLS + at + w],
                                                     start=(c == 0 and k == 0), stop=(c == C - 1 and k == 1))
                    t.then_inc(S["proj_a"], 1)
                if has(2):
                    turn_qk(n - 2, z_cross, "norm_b", "turn_b", "ev_a", n - 1)
                if has(4):
                    m = n - 4
                    need(pe, S["probs_ready"], m + 1)
                    need(pe, S["y_added"], m - 3)
                    for i in range(4):
                        t = nc.tensor.transpose(bank[6][:, i * P:(i + 1) * P], p_sb[:, (j - 4) % 4, i * P:(i + 1) * P], ident)
                    t.then_inc(S["pT_done2"], 1)
                if has(0):
                    need(pe, S["norm_b"], n - 1)
                    for c in range(C):
                        for k, part in enumerate((hi, lo)):
                            nc.tensor.matmul(bank_b[:, 0:256], xq[:, c * NVAR + 3, bt:bt + L],
                                             part[:, c * WCOLS + 512:c * WCOLS + 768],
                                             start=(c == 0 and k == 0), stop=(c == C - 1 and k == 1))
                    parts = [(c, a, w) for c in range(C) for a, w in ((0, hi), (0, lo), (1, hi))]
                    for i, (c, a, w) in enumerate(parts):
                        t = nc.tensor.matmul(bank_b[:, 256:512], ctx_hl[:, a, c, bt:bt + L],
                                             w[:, c * WCOLS + 768:c * WCOLS + 1024], start=(i == 0), stop=(i == len(parts) - 1))
                    t.then_inc(S["proj_b"], 1)
                if has(2):
                    m = n - 2
                    need(pe, S["exp2"], m)
                    need(pe, S["ev_b"], m + 1)
                    for i, t_in in enumerate((t_self, t_cross)):
                        for h in range(2):
                            at = (2 * i + h) * P
                            t = nc.tensor.matmul(bank[5][:, at:at + P], t_in[:, h, :], t_in[:, 2, :], start=True, stop=True)
                    t.then_inc(S["scores2"], 1)
                if has(7):
                    m = n - 7
                    part = ((j - 7) // B) % 2
                    need(pe, S["cat_ready"], m + 1)
                    if (j - 7) % B == 0:
                        g = g0 + (j - 7) // B
                        pe.wait_ge(S["w_hi_done"], WPIECES * (g + 1))
                        pe.wait_ge(S["w_lo_done"], WPIECES * (g + 1))
                    need(pe, S["pT_copied2"], min(m + 4, ITEMS) if isinstance(m, int) else m + 4)
                    if not has(4):
                        need(pe, S["y_added"], m)
                    for ch in range(4):
                        for k, w in enumerate((w_hi, w_lo)):
                            at = 2 * WCOLS + ch * D
                            t = nc.tensor.matmul(bank[6][:, 0:D], cat_q[:, (j - 7) % 2, ch, :], w[:, part, at:at + D],
                                                 start=(ch == 0 and k == 0), stop=(ch == 3 and k == 1))
                    t.then_inc(S["out_proj"], 1)
                if has(4):
                    m = n - 4
                    need(pe, S["pT_copied2"], m + 1)
                    need(pe, S["cat_raw"], m)
                    for i in range(2):
                        t = nc.tensor.matmul(bank[7][:, i * 256:(i + 1) * 256], v_ring[:, (j - 4) % 4, i, :],
                                             pT2[:, i * 256:(i + 1) * 256], start=True, stop=True)
                    t.then_inc(S["pv_done2"], 1)

            def x2_steps(j):
                b = j - 2
                if b == 0:
                    pe.wait_ge(S["norm_a"], ITEMS)
                    pe.wait_ge(S["norm_b"], ITEMS)
                if live(b, B):
                    pe.wait_ge(S["x2_ready"], b + 1)
                    need(pe, S["x2T_ready"], b - 1)
                    for c in range(C):
                        t = nc.tensor.transpose(bank[2 * (b % 2)][:, c * P:(c + 1) * P], x2_t[:, b % 2, c * P:(c + 1) * P], ident)
                    t.then_inc(S["x2_turned"], 1)
                b = j - 3
                if live(b, B):
                    pe.wait_ge(S["x2T_ready"], b + 1)
                    need(pe, S["logits_in"], b)
                    for c in range(C):
                        t = nc.tensor.matmul(bank[1][:, 0:E], x2T_t[:, b % 2, c, :], gate[:, c, :], start=(c == 0), stop=(c == C - 1))
                    t.then_inc(S["router"], 1)

            group_slots(pe, slot2, x2_steps)
            pe.wait_ge(S["logits_in"], B)
            x2p = (xq[:, 0:C, :], xq[:, C:2 * C, :])
            hp = hidden_parts()

            def slot3(m, j, e0):
                par = (j // 2) % 2
                tb = (j % 2) * 512
                for ic in range(IC):
                    if live(m, 2 * E):
                        if ic == 0 and isinstance(m, int) and m < 2:
                            pe.wait_ge(S["x2_hi"], (m + 1) * IC)
                            pe.wait_ge(S["x2_lo"], (m + 1) * IC)
                        if ic == 0 and j % 2 == 0:
                            e = e0 + j // 2
                            pe.wait_ge(S["w_hi_done"], WPIECES * (G + e + 1))
                            pe.wait_ge(S["w_lo_done"], WPIECES * (G + e + 1))
                        for k, free in ((0, "silu_done"), (1, "h_ready")):
                            need(pe, S[free], 4 * m + ic - 1)
                            to = bank[2 * k + ic % 2][:, :]
                            parts = [(c, a, w) for c in range(C) for a, w in ((0, w_hi), (0, w_lo), (1, w_hi))]
                            for i, (c, a, w) in enumerate(parts):
                                at = c * WCOLS + k * I + ic * P
                                t = nc.tensor.matmul(to, w[:, par, at:at + P], x2p[a][:, c, tb:tb + 512],
                                                     start=(i == 0), stop=(i == len(parts) - 1))
                        t.then_inc(S["gate_up"], 1)
                    if live(m - 1, 2 * E):
                        q, wp = (j - 1) % 2, ((j - 1) // 2) % 2
                        if ic == 0:
                            need(pe, S["h_hi"], 4 * m)
                            need(pe, S["h_lo"], 4 * m)
                        need(pe, S["acc_added"], 4 * (m - 2) + ic + 1)
                        parts = [(i, a, w) for i in range(IC) for a, w in ((0, w_hi), (0, w_lo), (1, w_hi))]
                        for k, (i, a, w) in enumerate(parts):
                            at = C * WCOLS + i * D
                            t = nc.tensor.matmul(bank[4 + ic][:, 0:D], hp[q][a][:, i, ic * L:(ic + 1) * L], w[:, wp, at:at + D],
                                                 start=(k == 0), stop=(k == len(parts) - 1))
                        t.then_inc(S["down_done"], 1)

            expert_slots(pe, slot3)

        @block.scalar
        def _(act):
            def high_piece(g, par, k, ready, count):
                act.wait_ge(S[ready], count)
                nc.scalar.activation(w_hi[:, par, k * PIECE:(k + 1) * PIECE], raw[:, k * PIECE:(k + 1) * PIECE],
                                     ACT.Copy).then_inc(S["w_hi_done"], 1)


            act.wait_ge(S["v_ones"], 1)
            nc.scalar.activation(warm[:, :], one16[:, 0:1], ACT.Exp)

            def exp_bank(m, j):
                need(act, S["neg_max1"], 4 * m + j + 1)
                need(act, S["pT_done1"], 4 * (m - 1) + j + 1)
                for h in range(4):
                    t = nc.scalar.activation(p_sb[:, j, h * P:(h + 1) * P], bank[2 + j % 2][:, h * P:(h + 1) * P], ACT.Exp,
                                             bias=neg_mx1[:, j, h:h + 1], scale=HD1 ** -0.5)
                t.then_inc(S["exp1"], 1)

            def copy_turned(m, j):
                need(act, S["pT_done1"], 4 * m + j + 1)
                if j == 0:
                    need(act, S["pv_done1"], m)
                nc.scalar.activation(pT1[:, j, :], bank[4 + j % 2][:, :], ACT.Copy).then_inc(S["pT_copied1"], 1)

            def slot1(n):
                a, b, z = n - 1, n - 2, n - 3
                if live(n, B):
                    if isinstance(n, int) and n == 0:
                        act.wait_ge(S["small_in"], 16)
                    need(act, S["qkv_done"], n + 1)
                    need(act, S["v_ready"], n)
                    need(act, S["turned1"], n)
                    nc.scalar.activation(qkv_raw[:, :], bank[0][:, 0:QKV1], ACT.Copy).then_inc(S["qkv_copied"], 1)
                if live(b, B):
                    copy_turned(b, 2)
                if live(a, B):
                    exp_bank(a, 0)
                if live(b, B):
                    copy_turned(b, 3)
                if live(a, B):
                    exp_bank(a, 1)
                    exp_bank(a, 2)
                if live(b, B):
                    need(act, S["oT_done"], b + 1)
                    need(act, S["attn_done"], b)
                    nc.scalar.activation(oT_sb[:, :, :].rearrange("p c l -> p (c l)"), bank[7][:, 0:D], ACT.Copy).then_inc(S["oT_copied"], 1)
                if live(a, B):
                    copy_turned(a, 0)
                if live(n, B):
                    need(act, S["turned1"], n + 1)
                    need(act, S["scores1"], 4 * n)
                    nc.scalar.activation(qT1[:, :, :].rearrange("p c l -> p (c l)"), bank[1][:, 0:D], ACT.Copy).then_inc(S["qT_ready"], 1)
                if live(z, B):
                    need(act, S["zT_done"], z + 1)
                    need(act, S["q_c"], z)
                    for c in range(C):
                        t = nc.scalar.activation(lnT[:, c, :], bank[0][:, c * P:(c + 1) * P], ACT.Identity,
                                                 scale=col["ln_w"][:, c:c + 1], bias=col["ln_b"][:, c:c + 1])
                    t.then_inc(S["zT_copied"], 1)
                if live(a, B):
                    exp_bank(a, 3)
                    copy_turned(a, 1)
                if isinstance(n, int) and n == 1:
                    for c, src in enumerate(context()):
                        act.wait_ge(S["ctx_in"], 32)
                        nc.scalar.activation(ctx_hl[:, 0, c, :], src, ACT.Copy).then_inc(S["ctx_hi"], 1)
                if isinstance(n, int) and n == 2:
                    for k in range(WPIECES):
                        high_piece(0, 0, k, "w_scaled", min(k + 1, SCALED))

            attention_slots(act, slot1)

            def slot2(n, j, g0):
                def has(k):
                    return live(n - k, ITEMS)

                def turned_qk(m, dst, at, turned, done):
                    need(act, S[turned], m + 1)
                    need(act, S["scores2"], m)
                    nc.scalar.activation(dst[:, 0:2, :].rearrange("p c l -> p (c l)"), bank[4][:, 0:2 * P], ACT.Identity,
                                         scale=col["qk_ln"][:, at:at + 1], bias=col["qk_ln"][:, at + 1:at + 2])
                    nc.scalar.activation(dst[:, 2, :], bank[4][:, 2 * P:3 * P], ACT.Identity,
                                         scale=col["qk_ln"][:, at + 2:at + 3], bias=col["qk_ln"][:, at + 3:at + 4]).then_inc(S[done], 1)

                def exp_heads(m, heads):
                    for h in heads:
                        t = nc.scalar.activation(p_sb[:, (j - 3) % 4, h * P:(h + 1) * P], bank[5][:, h * P:(h + 1) * P], ACT.Exp,
                                                 bias=neg_mx[:, h:h + 1], scale=DH ** -0.5, accum_out=sums[:, h:h + 1])
                    return t

                if has(3):
                    m = n - 3
                    need(act, S["neg_max2"], m + 1)
                    need(act, S["rden_ready"], m)
                    need(act, S["pT_done2"], m - 3)
                    exp_heads(m, (0, 1))
                if has(2):
                    turned_qk(n - 2, t_self, 0, "turn_a", "ev_a")
                if has(3):
                    exp_heads(n - 3, (2, 3)).then_inc(S["exp2"], 1)
                if has(2):
                    turned_qk(n - 2, t_cross, 4, "turn_b", "ev_b")
                if has(4):
                    m = n - 4
                    need(act, S["pT_done2"], m + 1)
                    need(act, S["pv_done2"], m)
                    nc.scalar.activation(pT2[:, :], bank[6][:, :], ACT.Copy).then_inc(S["pT_copied2"], 1)
                if has(5):
                    m = n - 5
                    part = ((j - 5) // B) % 2
                    need(act, S["pv_done2"], m + 1)
                    need(act, S["cat_m"], m)
                    for ch in range(4):
                        t = nc.scalar.activation(c_raw[:, ch * L:(ch + 1) * L], bank[7][:, ch * L:(ch + 1) * L], ACT.Copy,
                                                 scale=inv_smooth[:, part, ch:ch + 1])
                    t.then_inc(S["cat_raw"], 1)
                if has(1):
                    m = n - 1
                    part_b = bank[2 * ((j - 1) % 2) + 1]
                    need(act, S["nb_ready"], m + 1)
                    need(act, S["turn_b"], m)
                    for i in range(3):
                        t = nc.scalar.activation(z_cross[:, i, :], part_b[:, i * DH:(i + 1) * DH], ACT.Identity,
                                                 scale=rstd6[:, 3 + i:4 + i], bias=nb6[:, 3 + i:4 + i])
                    t.then_inc(S["norm_b"], 1)
                if j % B >= B - WPIECES and has(0):
                    g = g0 + j // B + 1
                    k = j % B - (B - WPIECES)
                    need(act, S["proj_b" if k < PROJ_PIECES else "out_proj"], (g - 1) * B)
                    high_piece(g, (j // B + 1) % 2, k, "w_scaled", g * SCALED + min(k + 1, SCALED))

            def x2_steps(j):
                b = j - 2
                if live(b, B):
                    act.wait_ge(S["x2_turned"], b + 1)
                    need(act, S["x2_lo"], b - 1)
                    need(act, S["router"], b - 1)
                    nc.scalar.activation(x2T_t[:, b % 2, :, :].rearrange("p c l -> p (c l)"), bank[2 * (b % 2)][:, 0:D],
                                         ACT.Copy).then_inc(S["x2T_ready"], 1)
                    act.wait_ge(S["x2T_ready"], b + 1)
                    nc.scalar.activation(xq[:, 0:C, b * L:(b + 1) * L], x2T_t[:, b % 2, :, :], ACT.Copy).then_inc(S["x2_hi"], 1)
                b = j - 3
                if live(b, B):
                    act.wait_ge(S["router"], b + 1)
                    nc.scalar.activation(logits[:, b * E:(b + 1) * E], bank[1][:, 0:E], ACT.Copy).then_inc(S["logits_in"], 1)

            group_slots(act, slot2, x2_steps)
            act.wait_ge(S["route_c"], 1)
            nc.scalar.activation(rt[:, 1, :], rt[:, 0, :], ACT.Exp).then_inc(S["comb_ready"], 1)
            hp = hidden_parts()

            def slot3(m, j, e0):
                if not live(m, 2 * E):
                    return
                for ic in range(IC):
                    need(act, S["gate_up"], 4 * m + ic + 1)
                    need(act, S["h_ready"], 4 * m + ic - 1)
                    nc.scalar.activation(s_sb[:, ic % 2, :], bank[ic % 2][:, :], ACT.Silu).then_inc(S["silu_done"], 1)
                    need(act, S["h_ready"], 4 * m + ic + 1)
                    if ic == 0:
                        need(act, S["down_done"], 4 * (m - 1))
                    nc.scalar.activation(hp[j % 2][0][:, ic, :], h_sb[:, ic % 2, :], ACT.Copy).then_inc(S["h_hi"], 1)
                    e1 = e0 + j // 2 + 1
                    k = next_piece(j, ic, e1)
                    if k is not None:
                        if k < PROJ_PIECES:
                            need(act, S["gate_up"], 4 * m)
                        else:
                            need(act, S["down_done"], 4 * (m - 1))
                        need(act, S["out_proj"], ITEMS)
                        high_piece(e1, (j // 2 + 1) % 2, k, "w_in", 16 * (G + e1 + 1))

            expert_slots(act, slot3)
            for b in range(1, B, 2):
                act.wait_ge(S["out_ready"], b + 1)
                act.dma_start(out[b], x_all[:, b * D:(b + 1) * D]).then_inc(S["out_done"], 16)

        @block.gpsimd
        def _(pool):
            nc.gpsimd.memset(one16[:, :], 1.0)
            nc.gpsimd.memset(neg_half[:, :], -0.5).then_inc(S["neg_ready"], 1)
            nc.gpsimd.memset(v_one[:, :], 1.0).then_inc(S["v_ones"], 1)
            pool.wait_ge(S["neg_ready"], 1)
            pool.wait_ge(S["v_ones"], 1)

            def low_piece(par, k, count):
                pool.wait_ge(S["w_hi_done"], count)
                a, b = k * PIECE, (k + 1) * PIECE
                nc.gpsimd.tensor_tensor(w_lo[:, par, a:b], raw[:, a:b], w_hi[:, par, a:b].bitcast(F32),
                                        ALU.subtract).then_inc(S["w_lo_done"], 1)

            def rsqrt(var, to, ready, done, count):
                pool.wait_ge(S[ready], count)
                nc.gpsimd.tensor_tensor(to, var, neg_half[:, 0:1], ALU.pow).then_inc(S[done], 1)

            def slot1(n):
                b, z, y = n - 2, n - 3, n - 4
                if live(n, B):
                    need(pool, S["qkv_copied"], n + 1)
                    nc.gpsimd.tensor_tensor(v_one[:, ds(n * 17, HD1)], qkv_raw[:, D + HD1:QKV1], one16[:, :], ALU.mult).then_inc(S["v_ready"], 1)
                if live(z, B):
                    for k in range(2):
                        rsqrt(ve[:, :], rstd[:, :], "var_ready", "rstd_ready", 2 * z + k + 1)
                if live(y, B):
                    need(pool, S["quant_ready"], y + 1)
                    nc.gpsimd.tensor_tensor(q_p[:, :], q_y[:, :], q_m[:, :], ALU.add).then_inc(S["qp_c"], 1)
                    need(pool, S["qp_c"], y + 1)
                    nc.gpsimd.tensor_tensor(xq[:, :, ds(y * L, L)], q_p[:, :].rearrange("p (v l) -> p v l", l=L),
                                            q_m[:, :].rearrange("p (v l) -> p v l", l=L), ALU.subtract).then_inc(S["xq_done"], 1)
                if live(b, B):
                    if isinstance(b, int) and b == 0:
                        pool.wait_ge(S["x_in"], 16)
                        pool.wait_ge(S["more_in"], 16)
                    need(pool, S["ax_ready"], b)
                    nc.gpsimd.tensor_tensor(xb[:, :], x_all[:, ds(b * D, D)], col["bo"], ALU.add).then_inc(S["xb_ready"], 1)
                if isinstance(n, int) and n == 1:
                    for c, src in enumerate(context()):
                        pool.wait_ge(S["ctx_hi"], c + 1)
                        pool.wait_ge(S["ctx_in"], 32)
                        nc.gpsimd.tensor_tensor(ctx_hl[:, 1, c, :], src, ctx_hl[:, 0, c, :].bitcast(F32), ALU.subtract).then_inc(S["ctx_lo"], 1)
                if isinstance(n, int) and 2 <= n <= LAG1:
                    half = WPIECES // 2
                    for k in range((n - 2) * half, (n - 1) * half):
                        low_piece(0, k, k + 1)

            attention_slots(pool, slot1, LAG1 + 1)

            def next_low(j, g0, k):
                low_piece((j // B + 1) % 2, k, (g0 + j // B + 1) * WPIECES + k + 1)

            def slot2(n, j, g0):
                def has(k):
                    return live(n - k, ITEMS)

                if has(1):
                    m = n - 1
                    need(pool, S["var2"], m + 1)
                    need(pool, S["norm_a"], m)
                    need(pool, S["norm_b"], m)
                    nc.gpsimd.tensor_tensor(rstd6[:, :], ag[:, 3, :], neg_half[:, 0:6], ALU.pow).then_inc(S["rstd2"], 1)
                if has(6):
                    m = n - 6
                    need(pool, S["cat_m"], m + 1)
                    nc.gpsimd.tensor_tensor(c_p[:, :], c_y[:, :], c_m[:, :], ALU.add).then_inc(S["cp_c"], 1)
                    need(pool, S["cp_c"], m + 1)
                    need(pool, S["out_proj"], m - 1)
                    nc.gpsimd.tensor_tensor(cat_q[:, (j - 6) % 2, :, :].rearrange("p c l -> p (c l)"), c_p[:, :], c_m[:, :],
                                            ALU.subtract).then_inc(S["cat_ready"], 1)
                if has(3):
                    m = n - 3
                    need(pool, S["exp2"], m + 1)
                    need(pool, S["rden_ready"], m + 1)
                    p = p_sb[:, (j - 3) % 4, :].rearrange("p (h t) -> p h t", h=4)
                    nc.gpsimd.tensor_tensor(p, p, rden2[:, :].unsqueeze(2).broadcast_to([P, 4, P]), ALU.mult).then_inc(S["probs_ready"], 1)
                if j % B == 0 and not (isinstance(n, int) and n == 0):
                    low_piece((j // B) % 2, WPIECES - 1, (g0 + j // B + 1) * WPIECES)
                if j % B > B - WPIECES and has(0):
                    next_low(j, g0, j % B - (B - WPIECES) - 1)

            def x2_steps(j):
                if live(j - 3, B):
                    x2_low(j - 3)
                if live(j, B):
                    pool.wait_ge(S["x2_var"], j + 1)
                    nc.gpsimd.tensor_tensor(rstd8[:, j:j + 1], ve8[:, j:j + 1], neg_half[:, 0:1], ALU.pow).then_inc(S["x2_rstd"], 1)

            def x2_low(b):
                pool.wait_ge(S["x2_hi"], b + 1)
                nc.gpsimd.tensor_tensor(xq[:, C:2 * C, b * L:(b + 1) * L], x2T_t[:, b % 2, :, :], xq[:, 0:C, b * L:(b + 1) * L].bitcast(F32),
                                        ALU.subtract).then_inc(S["x2_lo"], 1)

            group_slots(pool, slot2, x2_steps)
            hp = hidden_parts()

            def slot3(m, j, e0):
                if not live(m, 2 * E):
                    return
                for ic in range(IC):
                    need(pool, S["h_hi"], 4 * m + ic + 1)
                    if ic == 0:
                        need(pool, S["down_done"], 4 * (m - 1))
                    nc.gpsimd.tensor_tensor(hp[j % 2][1][:, ic, :], h_sb[:, ic % 2, :], hp[j % 2][0][:, ic, :].bitcast(F32),
                                            ALU.subtract).then_inc(S["h_lo"], 1)
                    e1 = e0 + j // 2 + 1
                    k = next_piece(j, ic, e1)
                    if k is not None:
                        low_piece((j // 2 + 1) % 2, k, (G + e1) * WPIECES + k + 1)

            expert_slots(pool, slot3)

            for half in range(2):
                pool.wait_ge(S["f_var"], half + 1)
                at = slice(half * IC, (half + 1) * IC)
                nc.gpsimd.tensor_tensor(rstd8[:, at], ve8[:, at], neg_half[:, 0:IC], ALU.pow).then_inc(S["f_rstd"], 1)

        @block.vector
        def _(dve):
            v = nc.vector
            dve.wait_ge(S["small_in"], 16)
            start = Chain(dve, S["consts"], 8, 0)
            v.tensor_copy(mask_b[:, :].rearrange("p (h t) -> p h t", h=4), col["mask"].unsqueeze(1).broadcast_to([P, 4, P])).then_inc(S["mask_ready"], 1)
            v.tensor_copy(ident_b[:, :], col["ident"]).then_inc(S["mask_ready"], 1)
            v.reciprocal(inv_in[:, :], col["in_scale"])
            start(v.memset(w_mul[:, G, :], 1.0))
            for c in range(C):
                t = v.tensor_tensor(w_mul[:, 0, c * NVAR:(c + 1) * NVAR], col["in_scale"][:, c * NVAR:(c + 1) * NVAR],
                                    col["w_scale"], ALU.mult)
            start(v.tensor_tensor(proj_c[:, :], col["proj"][:, 0:1], col["proj"][:, 1:2], ALU.mult))
            start(v.tensor_copy(w_mul[:, 1:G, :], w_mul[:, 0, :].unsqueeze(1).broadcast_to([P, G - 1, C * NVAR])))

            def scale_piece(g, par, k):
                dve.wait_ge(S["w_in"], 16 * (g + 1))
                if k < PROJ_PIECES:
                    c, half = divmod(k, 2)
                    for var, at, w in (((0, 0, 256), (1, 256, 128), (2, 384, 128)), ((3, 512, 256),))[half]:
                        a = c * WCOLS + at
                        mul = w_mul[:, :, :].rearrange("p g c -> p (g c)")[:, ds(g * C * NVAR + c * NVAR + var, 1)]
                        t = v.tensor_scalar(raw[:, a:a + w], raw[:, a:a + w], mul, None, ALU.mult)
                    t.then_inc(S["w_scaled"], 1)
                else:
                    v.reciprocal(inv_smooth[:, par, :], raw[:, WPIECES * PIECE:WALL]).then_inc(S["w_scaled"], 1)


            def top(m, j):
                need(dve, S["scores1"], 4 * m + j + 1)
                v.tensor_reduce(mx1[:, j, :], bank[2 + j % 2][:, :].rearrange("p (h t) -> p h t", h=4), AX, ALU.max).then_inc(S["max1"], 1)

            def minus_top(m, j):
                dve.wait_ge(S["max1"], 4 * m + j + 1)
                v.tensor_scalar(neg_mx1[:, j, :], mx1[:, j, :], -HD1 ** -0.5, None, ALU.mult).then_inc(S["neg_max1"], 1)

            cos, sin = (col[k].unsqueeze(1).broadcast_to([P, 17, ROT]) for k in ("cos", "sin"))
            heads = qkv_raw[:, 0:D + HD1].rearrange("p (h d) -> p h d", d=HD1)

            def slot1(n):
                a, b, z = n - 1, n - 2, n - 3
                if live(z, B):
                    x1 = x1_all[:, ds(z * D, D)]
                r1h, r2h = heads[:, :, 0:ROT], heads[:, :, ROT:2 * ROT]
                if live(z, B):
                    need(dve, S["attn_done"], z + 1)
                    need(dve, S["xb_ready"], z + 1)
                    v.tensor_tensor(ax[:, :], bank[7][:, 0:D], xb[:, :], ALU.add).then_inc(S["ax_ready"], 1)
                if live(a, B):
                    top(a, 0)
                if live(z, B):
                    dve.wait_ge(S["ax_ready"], z + 1)
                    v.bn_stats(bn[:, :], ax[:, :]).then_inc(S["ln_c"], 1)
                if live(a, B):
                    minus_top(a, 0)
                if live(n, B):
                    need(dve, S["qkv_copied"], n + 1)
                    v.tensor_tensor(rope_t[:, 0], r1h, cos, ALU.mult)
                    v.tensor_tensor(rope_t[:, 1], r2h, sin, ALU.mult)
                    v.tensor_tensor(rope_t[:, 2], r1h, sin, ALU.mult)
                    v.tensor_tensor(rope_t[:, 3], r2h, cos, ALU.mult).then_inc(S["rope_c"], 1)
                if live(z, B):
                    dve.wait_ge(S["ln_c"], 5 * z + 1)
                    settle()
                    v.bn_aggr(mv[:, :], bn[:, :]).then_inc(S["ln_c"], 1)
                if live(n, B):
                    dve.wait_ge(S["rope_c"], 2 * n + 1)
                    v.tensor_tensor(r1h, rope_t[:, 0], rope_t[:, 1], ALU.subtract)
                    v.tensor_tensor(r2h, rope_t[:, 2], rope_t[:, 3], ALU.add).then_inc(S["rope_c"], 1)
                if live(z, B):
                    dve.wait_ge(S["ln_c"], 5 * z + 2)
                    v.tensor_scalar(ve[:, :], mv[:, 1:2], EPS, None, ALU.add).then_inc(S["var_ready"], 1)
                if live(a, B):
                    top(a, 1)
                if live(n, B):
                    dve.wait_ge(S["rope_c"], 2 * n + 2)
                    v.tensor_copy(k_rep[:, :, :], qkv_raw[:, D:D + HD1].unsqueeze(1).broadcast_to([P, 8, HD1])).then_inc(S["roped"], 1)
                if live(a, B):
                    minus_top(a, 1)
                if live(z, B):
                    if isinstance(z, int) and z == 0:
                        dve.wait_ge(S["ctx_lo"], C)
                    dve.wait_ge(S["rstd_ready"], 2 * z + 1)
                    v.tensor_scalar(x1, ax[:, :], mv[:, 0:1], rstd[:, 0:1], ALU.subtract, ALU.mult).then_inc(S["ln_c"], 1)
                    dve.wait_ge(S["ln_c"], 5 * z + 3)
                    settle()
                    v.bn_stats(bn[:, :], x1).then_inc(S["ln_c"], 1)
                    dve.wait_ge(S["ln_c"], 5 * z + 4)
                    settle()
                    v.bn_aggr(mv[:, :], bn[:, :]).then_inc(S["ln_c"], 1)
                    dve.wait_ge(S["ln_c"], 5 * z + 5)
                    v.tensor_scalar(ve[:, :], mv[:, 1:2], EPS, None, ALU.add).then_inc(S["var_ready"], 1)
                if live(b, B):
                    need(dve, S["pv_done1"], b + 1)
                    need(dve, S["oT_done"], b)
                    o = bank[6][:, 0:17 * H1].rearrange("p (h d) -> p h d", d=17)
                    v.reciprocal(rden1[:, :], o[:, :, 16]).then_inc(S["rden_c"], 1)
                    dve.wait_ge(S["rden_c"], b + 1)
                    v.tensor_tensor(o_sb[:, :].rearrange("p (h d) -> p h d", d=HD1), o[:, :, 0:HD1],
                                    rden1[:, :].unsqueeze(2).broadcast_to([P, H1, HD1]), ALU.mult).then_inc(S["o_ready"], 1)
                if live(z, B):
                    need(dve, S["zT_done"], z)
                    dve.wait_ge(S["rstd_ready"], 2 * z + 2)
                    v.tensor_scalar(z2[:, :], x1, mv[:, 0:1], rstd[:, 0:1], ALU.subtract, ALU.mult).then_inc(S["z2_ready"], 1)
                if live(a, B):
                    top(a, 2)
                    minus_top(a, 2)
                    top(a, 3)
                    minus_top(a, 3)
                if live(n, B):
                    need(dve, S["turned1"], n + 1)
                    need(dve, S["qT_ready"], n + 1)
                    need(dve, S["scores1"], 4 * n)
                    v.tensor_tensor(k_bd[:, :, :], bank[1][:, D:D + P].unsqueeze(1).broadcast_to([P, 8, L]),
                                    col["head"].unsqueeze(2).broadcast_to([P, 8, L]), ALU.mult).then_inc(S["kbd_ready"], 1)
                if live(z, B):
                    need(dve, S["zT_copied"], z + 1)
                    need(dve, S["xq_done"], z)
                    y3 = q_y[:, :].rearrange("p (c v l) -> p c v l", c=C, v=NVAR)
                    v.tensor_tensor(y3, lnT[:, :, :].unsqueeze(2).broadcast_to([P, C, NVAR, L]),
                                    inv_in[:, :].rearrange("p (c v) -> p c v", c=C).unsqueeze(3).broadcast_to([P, C, NVAR, L]),
                                    ALU.mult).then_inc(S["q_c"], 1)
                    dve.wait_ge(S["q_c"], z + 1)
                    v.tensor_scalar(q_y[:, :], q_y[:, :], FP8_MAX, -FP8_MAX, ALU.min, ALU.max).then_inc(S["cq_c"], 1)
                    dve.wait_ge(S["cq_c"], z + 1)
                    v.tensor_scalar(q_m[:, :].bitcast(U16), q_y[:, :].bitcast(U16), NO_SIGN, None, ALU.bitwise_and).then_inc(S["abs_c"], 1)
                    dve.wait_ge(S["abs_c"], z + 1)
                    v.tensor_scalar(q_m[:, :], q_m[:, :], FP8_MIN_EXP, FP8_SHIFT, ALU.max, ALU.mult).then_inc(S["quant_ready"], 1)
                if isinstance(n, int) and n == 1:
                    for k in range(SCALED):
                        scale_piece(0, 0, k)

            attention_slots(dve, slot1)

            def add_output(n, j):
                m = n - 8
                b = (j - 8) % B
                need(dve, S["out_proj"], m + 1)
                if isinstance(m, int) and m < B:
                    v.tensor_copy(y_all[:, b, :], bank[6][:, 0:D]).then_inc(S["y_added"], 1)
                else:
                    need(dve, S["y_added"], m - B + 1)
                    v.tensor_tensor(y_all[:, b, :], bank[6][:, 0:D], y_all[:, b, :], ALU.add).then_inc(S["y_added"], 1)

            def slot2(n, j, g0):
                def has(k):
                    return live(n - k, ITEMS)

                if has(3):
                    m = n - 3
                    need(dve, S["scores2"], m + 1)
                    s = bank[5][:, :].rearrange("p (h t) -> p h t", h=4)
                    v.tensor_reduce(mx2[:, :], s, AX, ALU.max).then_inc(S["max2"], 1)
                if has(1):
                    m = n - 1
                    part_a, part_b = bank[2 * ((j - 1) % 2)], bank[2 * ((j - 1) % 2) + 1]
                    link = Chain(dve, S["agg_c"], 4, m)
                    need(dve, S["proj_a"], m + 1)
                    need(dve, S["nb_ready"], m)
                    for i in range(3):
                        v.bn_stats(st[:, i, :], part_a[:, i * DH:(i + 1) * DH])
                    if has(3):
                        dve.wait_ge(S["max2"], n - 3 + 1)
                        v.tensor_scalar(neg_mx[:, :], mx2[:, :], -DH ** -0.5, None, ALU.mult).then_inc(S["neg_max2"], 1)
                    need(dve, S["proj_b"], m + 1)
                    for i in range(3):
                        t = v.bn_stats(st[:, 3 + i, :], part_b[:, i * DH:(i + 1) * DH])
                    if has(8):
                        add_output(n, j)
                    link(t)
                    need(dve, S["rstd2"], m)
                    v.tensor_tensor(sum_m2[:, :, :], st[:, :, 1:3], st[:, :, 4:6], ALU.add)
                    link(v.tensor_tensor(ag[:, 0, :], st[:, :, 1], st[:, :, 4], ALU.subtract))
                    link(v.scalar_tensor_tensor(out=ag[:, 1, :], in0=ag[:, 0, :], scalar=DH / 4, in1=ag[:, 0, :],
                                                op0=ALU.mult, op1=ALU.mult))
                    need(dve, S["norm_a"], m)
                    v.tensor_scalar(mean6[:, :], sum_m2[:, :, 0], 0.5, None, ALU.mult)
                    link(v.tensor_tensor(ag[:, 2, :], ag[:, 1, :], sum_m2[:, :, 1], ALU.add))
                    v.tensor_scalar(ag[:, 3, :], ag[:, 2, :], 1.0 / DH, EPS, ALU.mult, ALU.add).then_inc(S["var2"], 1)
                if has(8) and not has(1):
                    add_output(n, j)
                if has(3) and not has(1):
                    dve.wait_ge(S["max2"], n - 3 + 1)
                    v.tensor_scalar(neg_mx[:, :], mx2[:, :], -DH ** -0.5, None, ALU.mult).then_inc(S["neg_max2"], 1)
                if has(6):
                    m = n - 6
                    need(dve, S["cat_raw"], m + 1)
                    need(dve, S["cat_ready"], m)
                    v.tensor_scalar(c_y[:, :], c_raw[:, :], FP8_MAX, -FP8_MAX, ALU.min, ALU.max).then_inc(S["cq_c"], 1)
                    dve.wait_ge(S["cq_c"], B + m + 1)
                    v.tensor_scalar(c_m[:, :].bitcast(U16), c_y[:, :].bitcast(U16), NO_SIGN, None, ALU.bitwise_and).then_inc(S["abs_c"], 1)
                    dve.wait_ge(S["abs_c"], B + m + 1)
                    v.tensor_scalar(c_m[:, :], c_m[:, :], FP8_MIN_EXP, FP8_SHIFT, ALU.max, ALU.mult).then_inc(S["cat_m"], 1)
                if has(1):
                    m = n - 1
                    need(dve, S["pv_done2"], m - 3)
                    v.tensor_copy(v_ring[:, (j - 1) % 4, 0, :], part_a[:, 3 * DH:4 * DH])
                    v.tensor_copy(v_ring[:, (j - 1) % 4, 1, :], part_b[:, 3 * DH:4 * DH])
                    need(dve, S["rstd2"], m + 1)
                    need(dve, S["norm_b"], m)
                    v.scalar_tensor_tensor(out=nb6[:, :], in0=sum_m2[:, :, 0], scalar=-0.5, in1=rstd6[:, :],
                                           op0=ALU.mult, op1=ALU.mult).then_inc(S["nb_ready"], 1)
                    need(dve, S["turn_a"], m)
                    for i in range(3):
                        t = v.tensor_scalar(z_self[:, i, :], part_a[:, i * DH:(i + 1) * DH], mean6[:, i:i + 1],
                                            rstd6[:, i:i + 1], ALU.subtract, ALU.mult)
                    t.then_inc(S["norm_a"], 1)
                if has(3):
                    m = n - 3
                    need(dve, S["exp2"], m + 1)
                    need(dve, S["probs_ready"], m)
                    v.reciprocal(rden2[:, :], sums[:, :]).then_inc(S["rden_ready"], 1)
                if B - WPIECES <= j % B < B - WPIECES + SCALED and has(0):
                    g = g0 + j // B + 1
                    k = j % B - (B - WPIECES)
                    if k == PROJ_PIECES:
                        need(dve, S["cat_raw"], (g - 1) * B)
                    scale_piece(g, (j // B + 1) % 2, k)

            def x2_stats(b):
                dve.wait_ge(S["y_added"], ITEMS - B + b + 1)
                link = Chain(dve, S["x2_c"], 3, b)
                y = y_all[:, b, :]
                link(v.scalar_tensor_tensor(out=y, in0=y, scalar=proj_c[:, 0:1], in1=x1_all[:, b * D:(b + 1) * D],
                                            op0=ALU.mult, op1=ALU.add))
                link(v.bn_stats(bn8[:, b, :], y))
                link(v.bn_aggr(mv8[:, b, :], bn8[:, b, :]))
                v.tensor_scalar(ve8[:, b:b + 1], mv8[:, b, 1:2], EPS, None, ALU.add).then_inc(S["x2_var"], 1)

            def x2_norm(b):
                dve.wait_ge(S["x2_rstd"], b + 1)
                need(dve, S["x2_turned"], b - 1)
                v.tensor_scalar(x2_t[:, b % 2, :], y_all[:, b, :], mv8[:, b, 0:1], rstd8[:, b:b + 1], ALU.subtract, ALU.mult).then_inc(S["x2_ready"], 1)
                v.tensor_scalar(x1_all[:, b * D:(b + 1) * D], y_all[:, b, :], mv8[:, b, 0:1], rstd8[:, b:b + 1],
                                ALU.subtract, ALU.mult).then_inc(S["x2_kept"], 1)

            def x2_steps(j):
                if live(j, B):
                    x2_stats(j)
                if live(j - 1, B):
                    x2_norm(j - 1)

            group_slots(dve, slot2, x2_steps)
            dve.wait_ge(S["x2_kept"], B)

            RC = Chain(dve, S["f_c"], 1000, 0)

            def be(i):
                return rt[:, i, :].rearrange("p (b e) -> p b e", b=B)

            def spread(i):
                return r1[:, i, :].unsqueeze(2).broadcast_to([P, B, E])

            lg = logits[:, :].rearrange("p (b e) -> p b e", b=B)
            rank = col["rank"].unsqueeze(1).broadcast_to([P, B, E])

            def route_probs():
                dve.wait_ge(S["logits_in"], B)
                RC(v.tensor_reduce(r1[:, 0, :], lg, AX, ALU.max))
                v.tensor_tensor(be(0), lg, spread(0), ALU.subtract).then_inc(S["route_c"], 1)
                dve.wait_ge(S["comb_ready"], 1)
                RC(v.tensor_reduce(r1[:, 1, :], be(1), AX, ALU.add))
                RC(v.reciprocal(r1[:, 2, :], r1[:, 1, :]))
                RC(v.tensor_tensor(be(2), be(1), spread(2), ALU.mult))
                RC(v.memset(be(7), 0.0))

            def route_top():
                RC(v.tensor_reduce(r1[:, 3, :], be(2), AX, ALU.max))
                RC(v.tensor_tensor(be(3), be(2), spread(3), ALU.is_equal))
                RC(v.tensor_tensor(be(4), be(3), rank, ALU.mult))
                RC(v.tensor_reduce(r1[:, 4, :], be(4), AX, ALU.max))
                RC(v.tensor_tensor(be(5), be(4), spread(4), ALU.is_equal))
                RC(v.tensor_tensor(be(6), be(5), be(2), ALU.mult))
                RC(v.tensor_tensor(be(7), be(7), be(6), ALU.add))
                RC(v.scalar_tensor_tensor(out=rt[:, 2, :], in0=rt[:, 5, :], scalar=-2.0, in1=rt[:, 2, :], op0=ALU.mult, op1=ALU.add))

            def route_weights():
                RC(v.tensor_reduce(r1[:, 0, :], be(7), AX, ALU.add))
                RC(v.reciprocal(r1[:, 1, :], r1[:, 0, :]))
                RC(v.tensor_tensor(comb[:, :, :], be(7), spread(1), ALU.mult))

            route_probs()
            route_top()

            comb_f = comb[:, :, :].rearrange("p b e -> p (b e)")

            def slot3(m, j, e0):
                for ic in range(IC):
                    if live(m, 2 * E):
                        need(dve, S["silu_done"], 4 * m + ic + 1)
                        need(dve, S["h_lo"], 4 * m + ic - 1)
                        need(dve, S["h_hi"], 4 * m + ic - 1)
                        v.tensor_tensor(h_sb[:, ic % 2, :], bank[2 + ic % 2][:, :], s_sb[:, ic % 2, :], ALU.mult).then_inc(S["h_ready"], 1)
                    if isinstance(m, int) and m == 0 and ic < 2:
                        (route_top, route_weights)[ic]()
                    if live(m - 1, 2 * E):
                        b = ((j - 1) % 2) * 4 + ic
                        if j == 0 and isinstance(e0, int):
                            at = b * E + e0 - 1
                        elif j == 0:
                            at = e0 + (b * E - 1)
                        else:
                            at = e0 + (b * E + (j - 1) // 2)
                        need(dve, S["down_done"], 4 * (m - 1) + ic + 1)
                        need(dve, S["acc_added"], 4 * (m - 3) + ic + 1)
                        if isinstance(m, int) and m - 1 < 2:
                            v.scalar_tensor_tensor(out=y_all[:, b, :], in0=bank[4 + ic][:, 0:D], scalar=comb_f[:, at:at + 1],
                                                   in1=x1_all[:, b * D:(b + 1) * D], op0=ALU.mult, op1=ALU.add).then_inc(S["acc_added"], 1)
                        else:
                            v.scalar_tensor_tensor(out=y_all[:, b, :], in0=bank[4 + ic][:, 0:D], scalar=comb_f[:, ds(at, 1)],
                                                   in1=y_all[:, b, :], op0=ALU.mult, op1=ALU.add).then_inc(S["acc_added"], 1)
                        if isinstance(m, int) and m >= 2 * E - 1:
                            stats = Chain(dve, S["out_c"], 2, b)
                            dve.wait_ge(S["acc_added"], 4 * (m - 1) + ic + 1)
                            stats(v.bn_stats(bn8[:, b, :], y_all[:, b, :]))
                            stats(v.bn_aggr(mv8[:, b, :], bn8[:, b, :]))

                if isinstance(m, int) and m >= 2 * E - 1:
                    output(m - (2 * E - 1))

            def output(half):
                at = slice(half * IC, (half + 1) * IC)
                v.tensor_scalar(ve8[:, at], mv8[:, at, 1], EPS, None, ALU.add).then_inc(S["f_var"], 1)
                dve.wait_ge(S["f_rstd"], half + 1)
                for b in range(half * IC, (half + 1) * IC):
                    v.tensor_scalar(x_all[:, b * D:(b + 1) * D], y_all[:, b, :], mv8[:, b, 0:1], rstd8[:, b:b + 1],
                                    ALU.subtract, ALU.mult).then_inc(S["out_ready"], 1)

            expert_slots(dve, slot3)


def _small(w):
    f = np.float32
    pos = np.arange(L, dtype=f)
    dims = 2 * ROT
    inv_freq = np.exp(-np.log(f(10000.0)) * (np.arange(0, dims, 2).astype(f) / f(dims)))
    theta = pos[:, None] * inv_freq[None, :]
    i, j = np.arange(L)[:, None], np.arange(L)[None, :]
    chunks = lambda a: np.asarray(a).reshape(C, P, -1).transpose(1, 0, 2).reshape(P, -1)
    spread = lambda a: np.broadcast_to(np.asarray(a).reshape(1, -1), (P, np.asarray(a).size))
    in_scale = np.stack([w[f"L0_xattn_{n}_in_scale"].reshape(C, P) for n in ("q", "k", "v", "qx")], axis=-1)
    cols = {
        "ident": np.eye(P, dtype=f),
        "mask": np.where((i - j >= 0) & (i - j < WINDOW), f(0), f(-1e9)),
        "cos": np.cos(theta), "sin": np.sin(theta),
        "head": (np.arange(P)[:, None] // HD1 == np.arange(8)[None, :]).astype(f),
        "ln_w": chunks(w["L0_xattn_ln_w"]), "ln_b": chunks(w["L0_xattn_ln_b"]),
        "in_scale": in_scale.transpose(1, 0, 2).reshape(P, C * NVAR),
        "qk_ln": np.stack([w[f"L0_xattn_{n}"] for n in ("qln_w", "qln_b", "kln_w", "kln_b", "qxln_w", "qxln_b", "kxln_w", "kxln_b")], axis=1),
        "w_scale": np.concatenate([spread(w[f"L0_xattn_{n}_scale"]) for n in ("wq", "wk", "wv", "wqx")], axis=1),
        "proj": np.concatenate([spread(w["L0_xattn_proj_w_scale"]), spread(w["L0_xattn_proj_in_scale"])], axis=1),
        "bo": spread(w["L0_attn_bo"]),
        "wqkv": chunks(np.concatenate([w["L0_attn_Wq"], w["L0_attn_Wk"], w["L0_attn_Wv"]], axis=1)),
        "wo": chunks(w["L0_attn_Wo"]),
        "gate": chunks(w["L0_ffn_gate_weight"].T),
        "rank": np.broadcast_to(np.arange(E, 0, -1).astype(f)[None], (P, E)),
    }
    return np.ascontiguousarray(np.concatenate([cols[k] for k in COL], axis=1))


def _weights(w):
    def grouped(a, per):
        return a.reshape(G, per * DH, C, P).transpose(0, 3, 2, 1)

    kx, vx = w["L0_xattn_w_kv_x"][:G * DH], w["L0_xattn_w_kv_x"][G * DH:]
    proj = np.concatenate([grouped(w["L0_xattn_wq"], 2), grouped(w["L0_xattn_wk"], 1), grouped(w["L0_xattn_wv"], 1),
                           grouped(w["L0_xattn_wqx"], 2), grouped(kx, 1), grouped(vx, 1)], axis=3).reshape(G, P, C * WCOLS)
    wp = w["L0_xattn_wproj"].T.reshape(2, G, 2, DH, D).transpose(1, 3, 0, 2, 4).reshape(G, P, 4 * D)
    smooth = w["L0_xattn_proj_smooth"].reshape(2, G, 2, DH).transpose(1, 3, 0, 2).reshape(G, P, 4)
    gu = w["L0_ffn_gate_up_proj"].reshape(E, 2 * I, C, P).transpose(0, 3, 2, 1).reshape(E, P, C * WCOLS)
    down = w["L0_ffn_down_proj"].reshape(E, D, IC, P).transpose(0, 3, 2, 1).reshape(E, P, IC * D)
    ones = np.ones((E, P, 4), np.float32)
    return np.ascontiguousarray(np.concatenate([np.concatenate([proj, wp, smooth], axis=2),
                                                np.concatenate([gu, down, ones], axis=2)], axis=0))


def kernel(**inputs):
    import concourse.bacc as _bacc
    from concourse.bass_utils import run_bass_kernel_spmd as _run

    w = {k: np.asarray(v) for k, v in inputs.items()}
    arrays = {
        "in_x": np.ascontiguousarray(w["x"]),
        "in_xT": np.ascontiguousarray(w["x"].reshape(B, L, C, P).transpose(0, 3, 2, 1)),
        "in_ctxT": np.ascontiguousarray(w["ctx_2048"].reshape(B * L, C, P).transpose(1, 2, 0)),
        "in_small": _small(w),
        "in_wall": _weights(w),
    }
    nc = _bacc.Bacc("TRN2", target_bir_lowering=False, num_devices=1)
    args = [nc.dram_tensor(k, a.shape, mybir.dt.from_np(a.dtype), kind="ExternalInput").ap() for k, a in arrays.items()]
    args.append(nc.dram_tensor("out", (B, L, D), F32, kind="ExternalOutput").ap())
    decoder_layer(nc, *args)
    r = _run(nc, [arrays], core_ids=[0])
    return r.results[0]["out"]
```
